# Optimizing a Trainium2 kernel written in Bass

```python
import numpy as np
import jax
import jax.numpy as jnp

def _softmax(x, axis=-1):
    return jax.nn.softmax(x, axis=axis)

def _gelu(x):
    return jax.nn.gelu(x, approximate=True)

def _silu(x):
    return jax.nn.silu(x)

def _sigmoid(x):
    return jax.nn.sigmoid(x)

def _layernorm(x, axis=-1, eps=1e-05):
    m = jnp.mean(x, axis=axis, keepdims=True)
    v = jnp.var(x, axis=axis, keepdims=True)
    return (x - m) / jnp.sqrt(v + eps)

def _scatter_add(tgt, idx, src, axis=0):
    return tgt.at[idx].add(src)

def _segment_sum(src, seg, n):
    return jax.ops.segment_sum(src, seg, n)
kernel_name = 'mk_flamingo_gated_d2_seqx_r4_613364'

def setup_inputs(seed: int=0):
    np.random.seed(seed)
    _w = jnp.asarray

    def _rec_inputs():
        import jax
        import jax.numpy as jnp
        _rk = jax.random.key(seed)
        x = 0.0001212 + 1 * jax.random.normal(jax.random.fold_in(_rk, 1), (8, 256, 512), jnp.float32)
        _lenS = 256 - jax.random.randint(jax.random.fold_in(_rk, 7), (8,), 0, max(1, 256 // 4) + 1, jnp.int32)
        _lenS2 = 256 - jax.random.randint(jax.random.fold_in(_rk, 8), (8,), 0, max(1, 256 // 4) + 1, jnp.int32)
        _ctx_2048P = jax.random.normal(jax.random.fold_in(_rk, 11), (8, 16, 512), jnp.float32)
        _ctx_2048c = jax.random.dirichlet(jax.random.fold_in(_rk, 511), 0.3 * jnp.ones((16,), jnp.float32), (8, 256))
        _ctx_2048t = jnp.einsum('bsk,bkd->bsd', _ctx_2048c, _ctx_2048P)
        _ctx_2048t = _ctx_2048t * jax.lax.rsqrt(jnp.mean(jnp.square(_ctx_2048t)) + 1e-12) * 0.953939
        ctx_2048 = 0.000173663 + 1.0001 * (_ctx_2048t + 0.3 * jax.random.normal(jax.random.fold_in(_rk, 611), (8, 256, 512), jnp.float32))
        _g = jax.random.normal(jax.random.fold_in(_rk, 9001), (2, 2), jnp.float32)
        _g = jnp.sign(_g) * jnp.maximum(jnp.abs(_g), 1.0) + (_g == 0) * 1.0
        g_xattn = _g[0]
        g_ffn = _g[1]
        return (x, ctx_2048, g_xattn, g_ffn)
    x, ctx_2048, g_xattn, g_ffn = _rec_inputs()

    def _L0_xattn_setup():
        import jax, jax.numpy as jnp
        import numpy as np
        B_DIM, T_DIM, C_DIM = (16, 256, 512)

        def _wkv(w, u, k, v):
            Bn, Tn, Cn = k.shape
            NEG_INF = jnp.float32(-1e+38)

            def step(carry, kv_t):
                p, q, o = carry
                kt, vt = kv_t
                no = jnp.maximum(o, u + kt)
                A = jnp.exp(o - no)
                E = jnp.exp(u + kt - no)
                y = (A * p + E * vt) / (A * q + E)
                no2 = jnp.maximum(w + o, kt)
                A2 = jnp.exp(w + o - no2)
                E2 = jnp.exp(kt - no2)
                return ((A2 * p + E2 * vt, A2 * q + E2, no2), y)
            init = (jnp.zeros((Bn, Cn), k.dtype), jnp.zeros((Bn, Cn), k.dtype), jnp.full((Bn, Cn), NEG_INF, k.dtype))
            kT = jnp.moveaxis(k, 1, 0)
            vT = jnp.moveaxis(v, 1, 0)
            _, yT = jax.lax.scan(step, init, (kT, vT))
            return jnp.moveaxis(yT, 0, 1)
        key = jax.random.key(seed)
        k1, k2, k3, k4 = jax.random.split(key, 4)
        w = -jnp.exp(jax.random.normal(k1, (C_DIM,), jnp.float32))
        u = jax.random.normal(k2, (C_DIM,), jnp.float32)
        k = jax.random.normal(k3, (B_DIM, T_DIM, C_DIM), jnp.float32)
        v = jax.random.normal(k4, (B_DIM, T_DIM, C_DIM), jnp.float32)
        return {'B': B_DIM, 'T': T_DIM, 'C': C_DIM, 'w': w, 'u': u, 'k': k, 'v': v}
    _L0_xattn_all = _L0_xattn_setup()
    _L0_xattn_in = {k: v for k, v in _L0_xattn_all.items() if k in ('w', 'u')}
    del _L0_xattn_all

    def _L0_ffn_setup():
        import jax, jax.numpy as jnp
        import numpy as np
        B, S, D, H = (4, 512, 512, 2048)

        def fwht(x):
            orig_shape = x.shape
            n = orig_shape[-1]
            x = x.reshape(-1, n)
            h = 1
            while h < n:
                xb = x.reshape(-1, n // (2 * h), 2, h)
                a = xb[:, :, 0, :]
                b = xb[:, :, 1, :]
                x = jnp.stack([a + b, a - b], axis=2).reshape(-1, n)
                h *= 2
            scale = jnp.asarray(1.0 / np.sqrt(n), dtype=x.dtype)
            return (x * scale).reshape(orig_shape)
        key = jax.random.key(seed)
        kx, k1, k2, k3 = jax.random.split(key, 4)
        x = jax.random.normal(kx, (B, S, D), dtype=jnp.float32)
        W1 = jax.random.normal(k1, (H, D), dtype=jnp.float32) * (1.0 / np.sqrt(D))
        W2 = jax.random.normal(k2, (D, H), dtype=jnp.float32) * (1.0 / np.sqrt(H))
        W3 = jax.random.normal(k3, (H, D), dtype=jnp.float32) * (1.0 / np.sqrt(D))
        return {'x': x, 'W1': W1, 'W2': W2, 'W3': W3}
    _L0_ffn_all = _L0_ffn_setup()
    _L0_ffn_in = {k: v for k, v in _L0_ffn_all.items() if k in ('W1', 'W2', 'W3')}
    del _L0_ffn_all

    def _L1_xattn_setup():
        import jax, jax.numpy as jnp
        import numpy as np

        def _wkv(time_decay, time_first, k, v):
            w = -jnp.exp(time_decay)
            u = time_first
            B, T, C = k.shape
            aa = jnp.zeros((B, C), dtype=k.dtype)
            bb = jnp.zeros((B, C), dtype=k.dtype)
            pp = jnp.full((B, C), -1e+38, dtype=k.dtype)

            def step(carry, kv_t):
                aa, bb, pp = carry
                kt, vt = kv_t
                ww = u + kt
                q = jnp.maximum(pp, ww)
                e1 = jnp.exp(pp - q)
                e2 = jnp.exp(ww - q)
                y_t = (e1 * aa + e2 * vt) / (e1 * bb + e2)
                ww2 = pp + w
                q2 = jnp.maximum(ww2, kt)
                e1b = jnp.exp(ww2 - q2)
                e2b = jnp.exp(kt - q2)
                new_carry = (e1b * aa + e2b * vt, e1b * bb + e2b, q2)
                return (new_carry, y_t)
            ks = jnp.transpose(k, (1, 0, 2))
            vs = jnp.transpose(v, (1, 0, 2))
            _, ys = jax.lax.scan(step, (aa, bb, pp), (ks, vs))
            return jnp.transpose(ys, (1, 0, 2))
        key = jax.random.key(seed)
        k1, k2, k3, k4 = jax.random.split(key, 4)
        B, T, C = (8, 256, 512)
        return {'batch_size': B, 'seq_len': T, 'embedding_dim': C, 'time_decay': jax.random.normal(k1, (C,), dtype=jnp.float32), 'time_first': jax.random.normal(k2, (C,), dtype=jnp.float32), 'k': jax.random.normal(k3, (B, T, C), dtype=jnp.float32), 'v': jax.random.normal(k4, (B, T, C), dtype=jnp.float32)}
    _L1_xattn_all = _L1_xattn_setup()
    _L1_xattn_in = {k: v for k, v in _L1_xattn_all.items() if k in ('time_decay', 'time_first')}
    del _L1_xattn_all

    def _L1_ffn_setup():
        import jax, jax.numpy as jnp
        import numpy as np
        B, S, H, I, E = (2, 128, 512, 1024, 8)
        JITTER_EPS = 0.01
        NEG_INF = float('-inf')

        def _route(logits):
            max1 = jnp.max(logits, axis=-1, keepdims=True)
            ind1 = jnp.argmax(logits, axis=-1, keepdims=True)
            factor1 = jnp.maximum(jnp.abs(logits), max1)
            mask1 = (max1 - logits) / factor1 > 2.0 * JITTER_EPS
            gates1 = jax.nn.softmax(jnp.where(mask1, NEG_INF, logits), axis=-1)
            mult1 = jnp.take_along_axis(gates1, ind1, axis=-1)
            sel1_onehot = jax.nn.one_hot(ind1[..., 0], E, dtype=jnp.bool_)
            masked_scores = jnp.where(sel1_onehot, NEG_INF, logits)
            max2 = jnp.max(masked_scores, axis=-1, keepdims=True)
            ind2 = jnp.argmax(masked_scores, axis=-1, keepdims=True)
            factor2 = jnp.maximum(jnp.abs(logits), max2)
            mask2 = (max2 - masked_scores) / factor2 > 2.0 * JITTER_EPS
            gates2 = jax.nn.softmax(jnp.where(mask2, NEG_INF, masked_scores), axis=-1)
            mult2 = jnp.take_along_axis(gates2, ind2, axis=-1)
            return (jnp.concatenate([mult1, mult2], axis=-1), jnp.concatenate([ind1, ind2], axis=-1))
        key = jax.random.key(seed)
        ks = jax.random.split(key, 5)
        std = 0.02
        return {'hidden_states': jax.random.normal(ks[0], (B, S, H), jnp.float32), 'gate_w': jax.random.normal(ks[1], (E, H), jnp.float32) * std, 'w1': jax.random.normal(ks[2], (E, I, H), jnp.float32) * std, 'w2': jax.random.normal(ks[3], (E, H, I), jnp.float32) * std, 'w3': jax.random.normal(ks[4], (E, I, H), jnp.float32) * std}
    _L1_ffn_all = _L1_ffn_setup()
    _L1_ffn_in = {k: v for k, v in _L1_ffn_all.items() if k in ('gate_w', 'w1', 'w2', 'w3')}
    del _L1_ffn_all
    return {'x': x, 'ctx_2048': ctx_2048, 'g_xattn': g_xattn, 'g_ffn': g_ffn, 'L0_xattn_w': _L0_xattn_in['w'], 'L0_xattn_u': _L0_xattn_in['u'], 'L0_ffn_W1': _L0_ffn_in['W1'], 'L0_ffn_W2': _L0_ffn_in['W2'], 'L0_ffn_W3': _L0_ffn_in['W3'], 'L1_xattn_time_decay': _L1_xattn_in['time_decay'], 'L1_xattn_time_first': _L1_xattn_in['time_first'], 'L1_ffn_gate_w': _L1_ffn_in['gate_w'], 'L1_ffn_w1': _L1_ffn_in['w1'], 'L1_ffn_w2': _L1_ffn_in['w2'], 'L1_ffn_w3': _L1_ffn_in['w3']}

def reference(x, ctx_2048, g_xattn, g_ffn, L0_xattn_w, L0_xattn_u, L0_ffn_W1, L0_ffn_W2, L0_ffn_W3, L1_xattn_time_decay, L1_xattn_time_first, L1_ffn_gate_w, L1_ffn_w1, L1_ffn_w2, L1_ffn_w3):
    import jax
    import jax.numpy as jnp

    def _L0_xattn_ref(B, T, C, w, u, k, v):
        import jax, jax.numpy as jnp
        import numpy as np
        B_DIM, T_DIM, C_DIM = (16, 256, 512)

        def _wkv(w, u, k, v):
            Bn, Tn, Cn = k.shape
            NEG_INF = jnp.float32(-1e+38)

            def step(carry, kv_t):
                p, q, o = carry
                kt, vt = kv_t
                no = jnp.maximum(o, u + kt)
                A = jnp.exp(o - no)
                E = jnp.exp(u + kt - no)
                y = (A * p + E * vt) / (A * q + E)
                no2 = jnp.maximum(w + o, kt)
                A2 = jnp.exp(w + o - no2)
                E2 = jnp.exp(kt - no2)
                return ((A2 * p + E2 * vt, A2 * q + E2, no2), y)
            init = (jnp.zeros((Bn, Cn), k.dtype), jnp.zeros((Bn, Cn), k.dtype), jnp.full((Bn, Cn), NEG_INF, k.dtype))
            kT = jnp.moveaxis(k, 1, 0)
            vT = jnp.moveaxis(v, 1, 0)
            _, yT = jax.lax.scan(step, init, (kT, vT))
            return jnp.moveaxis(yT, 0, 1)
        return _wkv(w, u, k, v)

    def _L0_ffn_ref(x, W1, W2, W3):
        import jax, jax.numpy as jnp
        import numpy as np
        B, S, D, H = (4, 512, 512, 2048)

        def fwht(x):
            orig_shape = x.shape
            n = orig_shape[-1]
            x = x.reshape(-1, n)
            h = 1
            while h < n:
                xb = x.reshape(-1, n // (2 * h), 2, h)
                a = xb[:, :, 0, :]
                b = xb[:, :, 1, :]
                x = jnp.stack([a + b, a - b], axis=2).reshape(-1, n)
                h *= 2
            scale = jnp.asarray(1.0 / np.sqrt(n), dtype=x.dtype)
            return (x * scale).reshape(orig_shape)
        up_gate = jnp.einsum('bsd,hd->bsh', x, W1)
        up_lin = jnp.einsum('bsd,hd->bsh', x, W3)
        hidden = jax.nn.silu(up_gate) * up_lin
        hidden = fwht(hidden)
        out = jnp.einsum('bsh,dh->bsd', hidden, W2)
        return out

    def _L1_xattn_ref(batch_size, seq_len, embedding_dim, time_decay, time_first, k, v):
        import jax, jax.numpy as jnp
        import numpy as np

        def _wkv(time_decay, time_first, k, v):
            w = -jnp.exp(time_decay)
            u = time_first
            B, T, C = k.shape
            aa = jnp.zeros((B, C), dtype=k.dtype)
            bb = jnp.zeros((B, C), dtype=k.dtype)
            pp = jnp.full((B, C), -1e+38, dtype=k.dtype)

            def step(carry, kv_t):
                aa, bb, pp = carry
                kt, vt = kv_t
                ww = u + kt
                q = jnp.maximum(pp, ww)
                e1 = jnp.exp(pp - q)
                e2 = jnp.exp(ww - q)
                y_t = (e1 * aa + e2 * vt) / (e1 * bb + e2)
                ww2 = pp + w
                q2 = jnp.maximum(ww2, kt)
                e1b = jnp.exp(ww2 - q2)
                e2b = jnp.exp(kt - q2)
                new_carry = (e1b * aa + e2b * vt, e1b * bb + e2b, q2)
                return (new_carry, y_t)
            ks = jnp.transpose(k, (1, 0, 2))
            vs = jnp.transpose(v, (1, 0, 2))
            _, ys = jax.lax.scan(step, (aa, bb, pp), (ks, vs))
            return jnp.transpose(ys, (1, 0, 2))
        assert seq_len <= 256
        return _wkv(time_decay, time_first, k, v)

    def _L1_ffn_ref(hidden_states, gate_w, w1, w2, w3):
        import jax, jax.numpy as jnp
        import numpy as np
        B, S, H, I, E = (2, 128, 512, 1024, 8)
        JITTER_EPS = 0.01
        NEG_INF = float('-inf')

        def _route(logits):
            max1 = jnp.max(logits, axis=-1, keepdims=True)
            ind1 = jnp.argmax(logits, axis=-1, keepdims=True)
            factor1 = jnp.maximum(jnp.abs(logits), max1)
            mask1 = (max1 - logits) / factor1 > 2.0 * JITTER_EPS
            gates1 = jax.nn.softmax(jnp.where(mask1, NEG_INF, logits), axis=-1)
            mult1 = jnp.take_along_axis(gates1, ind1, axis=-1)
            sel1_onehot = jax.nn.one_hot(ind1[..., 0], E, dtype=jnp.bool_)
            masked_scores = jnp.where(sel1_onehot, NEG_INF, logits)
            max2 = jnp.max(masked_scores, axis=-1, keepdims=True)
            ind2 = jnp.argmax(masked_scores, axis=-1, keepdims=True)
            factor2 = jnp.maximum(jnp.abs(logits), max2)
            mask2 = (max2 - masked_scores) / factor2 > 2.0 * JITTER_EPS
            gates2 = jax.nn.softmax(jnp.where(mask2, NEG_INF, masked_scores), axis=-1)
            mult2 = jnp.take_along_axis(gates2, ind2, axis=-1)
            return (jnp.concatenate([mult1, mult2], axis=-1), jnp.concatenate([ind1, ind2], axis=-1))
        b, s, h = hidden_states.shape
        x = hidden_states.reshape(-1, h)
        logits = x @ gate_w.T
        mult, sel = _route(logits)
        combine = jnp.einsum('tk,tke->te', mult, jax.nn.one_hot(sel, E, dtype=x.dtype))
        h1 = jnp.einsum('th,eih->eti', x, w1)
        h3 = jnp.einsum('th,eih->eti', x, w3)
        act = jax.nn.silu(h1) * h3
        y = jnp.einsum('eti,ehi->eth', act, w2)
        out = jnp.einsum('eth,te->th', y, combine)
        return out.reshape(b, s, h)
    x = x + jnp.tanh(g_xattn[0]) * _L0_xattn_ref(8, 256, 512, L0_xattn_w, L0_xattn_u, _layernorm(x, axis=-1), ctx_2048)
    x = x + jnp.tanh(g_ffn[0]) * _L0_ffn_ref(_layernorm(x, axis=-1), L0_ffn_W1, L0_ffn_W2, L0_ffn_W3)
    x = x + jnp.tanh(g_xattn[1]) * _L1_xattn_ref(8, 256, 512, L1_xattn_time_decay, L1_xattn_time_first, _layernorm(x, axis=-1), ctx_2048)
    x = x + jnp.tanh(g_ffn[1]) * _L1_ffn_ref(_layernorm(x, axis=-1), L1_ffn_gate_w, L1_ffn_w1, L1_ffn_w2, L1_ffn_w3)
    return x

_drawn_inputs = setup_inputs


def setup_inputs(seed=0):
    import zlib

    import numpy as np

    out = dict(_drawn_inputs(seed))
    spreads = {'g_ffn': (-1.0, 0.2)}
    factors = {}
    for name, (base, spread) in spreads.items():
        noise = np.random.default_rng([zlib.crc32(name.encode()), seed]).standard_normal(out[name].shape)
        drawn = base * np.exp(spread * noise) if base else spread * noise
        out[name] = jnp.asarray(drawn.astype(out[name].dtype))
    for name, factor in factors.items():
        out[name] = (out[name] * factor).astype(out[name].dtype)
    return out
```

```python
from contextlib import ExitStack

import concourse.bass as bass
from concourse import mybir

F32 = mybir.dt.float32
F16 = mybir.dt.float16
I32 = mybir.dt.int32
ALU = mybir.AluOpType
ACT = mybir.ActivationFunctionType
AX = mybir.AxisListType.X

P = 128
BATCH, T, D = 8, 256, 512
TOK = BATCH * T
NT = 512
NG = TOK // NT
NB = NT // T
C = D // P
W = C * NT
H = 2048
J = H // P
E, I = 8, 1024
IC = I // P
TILES = NT // P
EPS = 1e-5
JITTER2 = 0.02

SW = 256.0
SX = 64.0
SH = 16.0

SLOTS = 2 * TOK // P + E - 1
SPARE = (SLOTS - 2 * TOK // P) * P
LIST = E * TOK + SPARE + P
EXPERT = 2 * C * I + IC * D
ADD, SUB, MUL, MAXO = ALU.add, ALU.subtract, ALU.mult, ALU.max

BRANCHES = [("pre", 0)]
for _g in range(NG):
    if _g + 1 < NG:
        BRANCHES.append(("pre", _g + 1))
    if _g >= 1:
        BRANCHES.append(("post", _g - 1))
BRANCHES.append(("post", NG - 1))
NORMS = [(k, g, i) for k, g in BRANCHES for i in range(2 if k == "pre" else 1)]

PRE_STEPS = ["sums", "var", "norm", "exps", "mix", "sums2", "var2", "norm2"]
POST_STEPS = ["sums", "var", "norm", "exps", "mix", "rows", "gate", "rank"]


def branch_index(kind, g):
    return BRANCHES.index((kind, g))


def norm_index(kind, g, i):
    return NORMS.index((kind, g, i))


def steps_beside(g, j):
    if j < 8:
        return ("pre", g + 1, PRE_STEPS[j]) if g + 1 < NG else None
    return ("post", g - 1, POST_STEPS[j - 8]) if g >= 1 else None


def build(nc, x_cm, ctx_cm, vecs, gains, w1t, w3t, w2t, gate_t, e13, e2, had, ones_mean, ident,
          tri, ones16, tok_id, ebase, desc, blocks, slot_no, out):
    ctx = ExitStack()
    with ctx:
        def sb(name, shape, dt):
            return ctx.enter_context(nc.sbuf_tensor(name, shape, dt))

        def sem(name):
            return ctx.enter_context(nc.semaphore(name))

        xn_rows = nc.dram_tensor("xn_rows", (TOK, D), F32).ap()
        x3_rows = nc.dram_tensor("x3_rows", (TOK, D), F32).ap()
        row_list = nc.dram_tensor("row_list", (LIST, 1), I32).ap()
        y_rows = nc.dram_tensor("y_rows", (SLOTS * P, D), F32).ap()

        weights = sb("weights", [P, 2 * EXPERT], F32)
        w16 = weights[:, :].bitcast(F16)
        n1 = 2 * C * H
        w1s = w16[:, 0:n1].rearrange("p (s c h) -> p s c h", s=2, c=C)
        w3s = w16[:, n1:2 * n1].rearrange("p (s c h) -> p s c h", s=2, c=C)
        w2s = w16[:, 2 * n1:2 * n1 + 2 * J * D].rearrange("p (s j d) -> p s j d", s=2, j=J)
        X = sb("X", [P, 3, C, NT], F32)
        V = sb("V", [P, W], F32)
        K = sb("K", [P, W], F32)
        E1 = sb("E1", [P, W], F32)
        E2 = sb("E2", [P, W], F32)
        SPs = sb("SPs", [P, W], F32)
        SQs = sb("SQs", [P, W], F32)
        xs = sb("xs", [P, 2, 2, C, NT], F16)
        sg = sb("sg", [P, 2, NT], F32)
        hid = sb("hid", [P, 2, NT], F32)
        hs = sb("hs", [P, 2, 2, NT], F16)
        vec = sb("vec", [P, 4, C], F32)
        dec = sb("dec", [P, 2, C], F32)
        nm = sb("nm", [P, 2, C], F32)
        um = sb("um", [P, 2, C], F32)
        gn = sb("gn", [P, 4], F32)
        sc = sb("sc", [P, 4], F32)
        eps = sb("eps", [P, 1], F32)
        one = sb("one", [P, 1], F32)
        hads = sb("hads", [P, 2, P], F16)
        onesm = sb("onesm", [P, P], F32)
        idn = sb("idn", [P, P], F32)
        tris = sb("tris", [P, P], F16)
        ones1 = sb("ones1", [P, P], F16)
        gw = sb("gw", [P, C, E], F32)
        gsum = sb("gsum", [P, E], F32)
        tid = sb("tid", [P, TOK // P], I32)
        ebs = sb("ebs", [P, E], F32)
        dsc = sb("dsc", [P, E], F32)
        blk = sb("blk", [P, 16], F32)
        sno = sb("sno", [P, SLOTS + 1], F32)
        zero = sb("zero", [P, LIST // P], I32)
        st = sb("st", [P, TILES, 6], F32)
        mv = sb("mv", [P, TILES, 2], F32)
        rt = sb("rt", [P, 4, TILES], F32)
        q = [sb(f"q{n}", [P, TILES, E], F32) for n in range(10)]
        r4 = [sb(f"r4_{n}", [P, TILES], F32) for n in range(6)]
        a16 = sb("a16", [P, 2, TILES, E], F16)
        cum = sb("cum", [P, E], F32)
        mult = sb("mult", [P, 2, TOK // P], F32)
        pos = sb("pos", [P, 2, TOK // P], I32)
        ypos = sb("ypos", [P, 2, TOK // P], I32)
        posf = sb("posf", [P, 2 * TOK // P, 1 + E], F32)
        cnt = sb("cnt", [P, 6, E], F32)
        cmp16 = sb("cmp16", [P, E, 16], F32)
        sl = sb("sl", [P, 4, SLOTS + 1], F32)
        sle = sb("sle", [P, SLOTS + 1, E], F32)
        table = sb("table", [P, 4, SLOTS + 1], I32)
        starts = sb("starts", [P, E], I32)

        PS = ctx.enter_context(nc.psum_tensor("PS", [P, 8, NT], F32))
        bank = lambda n: PS[:, n, :]
        ABANK, BBANK, OUT0, S0, S1 = 0, 1, 2, 6, 7

        names = """const_in hot_in gains_th scal_ready decay_a dec_ready gsum_ready gmean_ready gw_ready zeroed
            stage_scaled stage_bfly stage_hi stage_lo had_out had_hi had_lo zero_set list_zero
            v_in v_used sq_done sums_done stat_done msq_done var_done r0_done k_done xh_done xs_ready
            e1_done e2_done ev1_done ev2_done q_done den_done rec_done wkv_done
            a_done b_done sig_done s_done hid_done hh_done hl_done down_done out_done resid_done
            lg_done tr_done xt_done raw_done tvar_done tr0_done xn_done x3_out xn_out d_done ex_done
            asg_done rank_done pos_done scat_done cum_done count_done table_done
            idx_in rows_in xT_done xT_used up_done act_done slot_down aT_done aT_used y_out
            y_ready gathers g1_done sil_done sig_steps vchain achain gchain c_out""".split()
        s = {n: sem(n) for n in names}
        x_in = [sem(f"x_in{n}") for n in range(3)]
        st_in = [sem(f"st_in{n}") for n in range(2)]
        wl = sem("expert_in")
        idx_s = [sem(f"idx_in{n}") for n in range(2)]
        row_s = [sem(f"rows_in{n}") for n in range(2)]
        ysto = [sem(f"y_store{n}") for n in range(2)]
        c_x3 = [sem(f"c_x3_{n}") for n in range(2)]
        c_y = [sem(f"c_y_{n}") for n in range(2)]
        c_st = [sem(f"c_st_{n}") for n in range(2)]

        xg = lambda g: X[:, g % 3, :, :].rearrange("p c n -> p (c n)")
        ch = lambda t, c: t[:, c * NT:(c + 1) * NT]
        seq = lambda t: t[:, :].rearrange("p (a t) -> p a t", t=T)
        later = lambda t: seq(t)[:, :, 1:T]
        before = lambda t: seq(t)[:, :, 0:T - 1]
        wide = lambda t: t.rearrange("p (o n) -> p o n", o=1).to_broadcast([P, C, NT])
        cn = lambda t: t.rearrange("p (c n) -> p c n", c=C)
        M_, MSQ, VAR, RS = (E1[:, n * NT:(n + 1) * NT] for n in range(4))
        stage = [X[:, 1 + n, :, :].rearrange("p c n -> p (c n)") for n in range(2)]
        UNITS = 2 * C + 4
        blockv = ctx.enter_context(nc.Block())

        def unit_src(u):
            if u < C:
                return w1t[:, u, :]
            if u < 2 * C:
                return w3t[:, u - C, :]
            j = 4 * (u - 2 * C)
            return w2t[:, j:j + 4, :].rearrange("p j d -> p (j d)")

        def unit_dst(u, half):
            if u < C:
                return w1s[:, half, u, :]
            if u < 2 * C:
                return w3s[:, half, u - C, :]
            j = 4 * (u - 2 * C)
            return w2s[:, half, j:j + 4, :].rearrange("p j d -> p (j d)")

        unit_slot = lambda u: u % 2 if u < 2 * C else 0
        def unit_loads(u):
            return sum(unit_slot(v) == unit_slot(u) for v in range(u + 1))

        CONSTS = [(hads[:, :, :], had), (idn[:, :], ident), (tris[:, :], tri), (ones1[:, :], ones16),
                  (tid[:, :], tok_id), (ebs[:, :], ebase), (dsc[:, :], desc), (blk[:, :], blocks),
                  (sno[:, :], slot_no), (gw[:, :, :], gate_t)]
        posts_before = lambda b: sum(kind == "post" for kind, _ in BRANCHES[:b])

        grow = [SPs[:, n * D:(n + 1) * D] for n in range(2)]
        xTt = [SPs[:, (2 + n) * D:(3 + n) * D].rearrange("p (c n) -> p c n", c=C) for n in range(2)]
        sil = [K[:, 0:I], K[:, I:2 * I]]
        aTt = [SQs[:, n * I:(n + 1) * I].rearrange("p (c n) -> p c n", c=IC) for n in range(2)]
        yt = [V[:, n * D:(n + 1) * D] for n in range(2)]
        idxt = sb("idxt", [P, 2], I32)
        cx3 = [E1[:, n * D:(n + 1) * D] for n in range(2)]
        cy = [[E2[:, (2 * n + k) * D:(2 * n + k + 1) * D] for k in range(2)] for n in range(2)]

        @blockv.sync
        def _(sp):
            def load_v(b):
                if b >= 1:
                    sp.wait_ge(s["v_used"], b)
                sp.dma_start(V[:, :], ctx_cm[BRANCHES[b][1], :, :]).then_inc(s["v_in"], 16)

            def load_x(g):
                if g in (1, 2):
                    sp.wait_ge(s["stage_lo"], UNITS)
                if g >= 3:
                    sp.wait_ge(s["tr_done"], TILES * (g - 2))
                sp.dma_start(xg(g), x_cm[g, :, :]).then_inc(x_in[g % 3], 16)

            sp.dma_start(vec[:, :, :], vecs).then_inc(s["hot_in"], 16)
            sp.dma_start(gn[:, :], gains).then_inc(s["hot_in"], 16)
            sp.dma_start(onesm[:, :], ones_mean).then_inc(s["hot_in"], 16)
            load_x(0)
            load_v(0)
            for t, a in CONSTS:
                sp.dma_start(t, a).then_inc(s["const_in"], 16)
            for u in range(UNITS):
                if u >= 1 and unit_slot(u) == 0 and u > 2 * C:
                    sp.wait_ge(s["stage_lo"], u)
                elif u >= 2:
                    sp.wait_ge(s["stage_lo"], u - 1)
                sp.dma_start(stage[unit_slot(u)], unit_src(u)).then_inc(st_in[unit_slot(u)], 16)
            sp.wait_ge(s["zero_set"], 1)
            sp.dma_start(row_list.rearrange("(p n) o -> p (n o)", p=P), zero[:, :]).then_inc(s["list_zero"], 16)
            load_x(1)
            for b in range(1, len(BRANCHES)):
                load_v(b)
                kind, g = BRANCHES[b]
                if kind == "pre" and g + 1 < 3:
                    load_x(g + 1)
                if kind == "post":
                    sp.wait_ge(s["xt_done"], TILES * (g + 1))
                    sp.dma_start(x3_rows[g * NT:(g + 1) * NT, :].rearrange("(i p) d -> p i d", p=P), cn(E1[:, :])).then_inc(s["x3_out"], 16)
                    if g + 3 < NG:
                        load_x(g + 3)
                    sp.wait_ge(s["xn_done"], g + 1)
                    sp.dma_start(xn_rows[g * NT:(g + 1) * NT, :].rearrange("(i p) d -> p i d", p=P), cn(K[:, :])).then_inc(s["xn_out"], 16)
            sp.wait_ge(s["down_done"], NG * J)
            wreg = weights[:, :].rearrange("p (b n) -> p b n", b=2)
            sp.wait_ge(s["table_done"], 1)
            for e in range(E):
                if e >= 1:
                    sp.wait_ge(wl, 32 * e)
                if e >= 2:
                    first = sp.value_load(starts[0:1, e - 2:e - 1], min_val=1, max_val=SLOTS + 1)
                    sp.wait_ge(s["slot_down"], first)
                sp.dma_start(wreg[:, e % 2, 0:2 * C * I], e13[e, :, :]).then_inc(wl, 16)
                sp.dma_start(wreg[:, e % 2, 2 * C * I:EXPERT], e2[e, :, :]).then_inc(wl, 16)
            x3v = x3_rows.rearrange("(i p) d -> i p d", p=P)
            outv = out.rearrange("(i p) d -> i p d", p=P)

            def load_x3(i):
                if i >= 2:
                    sp.wait_ge(c_st[i % 2], 16 * (i // 2))
                sp.dma_start(cx3[i % 2], x3v[i, :, :]).then_inc(c_x3[i % 2], 16)

            sp.wait_ge(s["x3_out"], 16 * NG)
            load_x3(0)
            load_x3(1)
            for i in range(TOK // P):
                sp.wait_ge(s["c_out"], i + 1)
                sp.dma_start(outv[i, :, :], cx3[i % 2]).then_inc(c_st[i % 2], 16)
                if i + 2 < TOK // P:
                    load_x3(i + 2)
            for n in range(2):
                sp.wait_ge(c_st[n], 16 * (TOK // P // 2))

        @blockv.gpsimd
        def _(gp):
            chain = [0]

            def link(ins):
                chain[0] += 1
                ins.then_inc(s["gchain"], 1)
                gp.wait_ge(s["gchain"], chain[0])

            gp.memset(zero[:, :], 0).then_inc(s["zero_set"], 1)

            def split(u):
                a = stage[unit_slot(u)]
                gp.wait_ge(s["stage_scaled"], u + 1)
                if u >= 2 * C:
                    if u == 2 * C:
                        gp.wait_ge(s["stage_lo"], u)
                    b4 = stage[1].rearrange("p (b a d) -> p b a d", b=2, a=2)
                    a4 = a.rearrange("p (b a d) -> p b a d", b=2, a=2)
                    link(gp.tensor_tensor(b4[:, :, 0, :], a4[:, :, 0, :], a4[:, :, 1, :], ADD))
                    link(gp.tensor_tensor(b4[:, :, 1, :], a4[:, :, 0, :], a4[:, :, 1, :], SUB))
                    link(gp.tensor_tensor(a[:, 0:2 * D], stage[1][:, 0:2 * D], stage[1][:, 2 * D:4 * D], ADD))
                    gp.tensor_tensor(a[:, 2 * D:4 * D], stage[1][:, 0:2 * D], stage[1][:, 2 * D:4 * D], SUB).then_inc(s["stage_bfly"], 1)
                gp.wait_ge(s["stage_hi"], u + 1)
                gp.tensor_tensor(unit_dst(u, 1), a, unit_dst(u, 0), SUB).then_inc(s["stage_lo"], 1)

            def products(b):
                gp.wait_ge(s["v_in"], 16 * (b + 1))
                gp.wait_ge(s["e1_done"], b + 1)
                gp.wait_ge(s["e2_done"], b + 1)
                gp.tensor_tensor(K[:, :], E1[:, :], V[:, :], MUL).then_inc(s["ev1_done"], 1)
                gp.wait_ge(s["q_done"], b + 1)
                gp.wait_ge(s["ev1_done"], b + 1)
                gp.tensor_tensor(E1[:, :], E2[:, :], V[:, :], MUL).then_inc(s["ev2_done"], 1)

            def scatter(g):
                gp.wait_ge(s["list_zero"], 16)
                gp.wait_ge(s["pos_done"], g + 1)
                gp.wait_ge(s["const_in"], 16 * len(CONSTS))
                for i in range(g * TILES, (g + 1) * TILES):
                    for k in range(2):
                        gp.indirect_dma_start(row_list, bass.IndirectOffsetOnAxis(ap=pos[:, k, i:i + 1], axis=0),
                                              tid[:, i:i + 1], None).then_inc(s["scat_done"], 16)

            for u in range(4):
                split(u)
            products(0)
            for u in range(4, UNITS):
                split(u)
            for g in range(NG):
                for j in range(J):
                    step = steps_beside(g, j)
                    if step and step[2] == "exps":
                        products(branch_index(step[0], step[1]))
                    if step and step[2] == "rank":
                        scatter(step[1])
            products(branch_index("post", NG - 1))
            scatter(NG - 1)

            gp.wait_ge(s["table_done"], 1)
            gp.wait_ge(s["scat_done"], 16 * 2 * TOK // P)
            gp.wait_ge(s["xn_out"], 16 * NG)
            gp.wait_ge(s["wkv_done"], len(BRANCHES))

            def first_row(i):
                return gp.value_load(table[0:1, 2, bass.ds(i, 1)], min_val=0, max_val=LIST - P)

            def load_list(i, n, par):
                gp.dma_start(idxt[:, par:par + 1], row_list[bass.ds(first_row(i), P), :]).then_inc(idx_s[par], 16)

            def gather(i, n, par):
                gp.wait_ge(idx_s[par], 16 * n)
                gp.sem_inc(s["gathers"], 1)
                gp.indirect_dma_start(grow[par], None, xn_rows, bass.IndirectOffsetOnAxis(ap=idxt[:, par:par + 1], axis=0)).then_inc(row_s[par], 16)

            def store(i, n, par):
                gp.wait_ge(s["y_ready"], i + 2)
                gp.dma_start(y_rows[bass.ds(i * P, P), :], yt[par]).then_inc(ysto[par], 16)

            load_list(0, 1, 0)
            load_list(1, 1, 1)
            gather(0, 1, 0)
            gather(1, 1, 1)

            def block(i, n, par):
                gp.wait_ge(row_s[par], 16 * n)
                load_list(i + 2, n + 1, par)
                gp.wait_ge(s["xT_done"], i + 1)
                gather(i + 2, n + 1, par)
                store(i, n, par)

            with gp.Fori(0, (SLOTS - 1) // 2, 1) as m:
                block(2 * m, m + 1, 0)
                block(2 * m + 1, m + 1, 1)
            n = (SLOTS - 1) // 2
            store(2 * n, n + 1, 0)
            gp.wait_ge(row_s[0], 16 * (n + 1))
            gp.wait_ge(row_s[1], 16 * (n + 1))
            for k in range(2):
                gp.wait_ge(ysto[k], 16 * (n + 1 - k))
            for i in range(TOK // P):
                if i >= 2:
                    gp.wait_ge(s["c_out"], i - 1)
                for k in range(2):
                    gp.indirect_dma_start(cy[i % 2][k], None, y_rows, bass.IndirectOffsetOnAxis(ap=ypos[:, k, i:i + 1], axis=0)).then_inc(c_y[i % 2], 16)

        @blockv.scalar
        def _(act):
            chain = [0]

            def link(ins):
                chain[0] += 1
                ins.then_inc(s["achain"], 1)
                act.wait_ge(s["achain"], chain[0])

            act.wait_ge(s["hot_in"], 48)
            act.activation(gn[:, :], gn[:, :], ACT.Tanh).then_inc(s["gains_th"], 1)
            act.preload_act_table_set("natural_log_exp_and_others")
            act.wait_ge(s["zeroed"], 2)
            link(act.activation(vec[:, 2, :], vec[:, 2, :], ACT.Exp))
            act.activation(dec[:, 0, :], vec[:, 0, :], ACT.Exp)
            act.activation(dec[:, 1, :], vec[:, 2, :], ACT.Exp, scale=-1.0).then_inc(s["dec_ready"], 1)

            def scale_unit(u):
                sl_ = unit_slot(u)
                act.wait_ge(st_in[sl_], 16 * unit_loads(u))
                act.activation(stage[sl_], stage[sl_], ACT.Copy, scale=SW).then_inc(s["stage_scaled"], 1)

            def high_unit(u):
                act.wait_ge(s["stage_scaled"], u + 1)
                if u >= 2 * C:
                    act.wait_ge(s["stage_bfly"], u - 2 * C + 1)
                act.activation(unit_dst(u, 0), stage[unit_slot(u)], ACT.Copy).then_inc(s["stage_hi"], 1)

            def had_high(jj):
                act.wait_ge(s["had_out"], jj + 1)
                for a in range(4):
                    ins = act.activation(w2s[:, 0, 4 * a + jj, :], bank(OUT0 + a), ACT.Copy, scale=float(H) ** -0.5)
                ins.then_inc(s["had_hi"], 1)

            def run(kind, g, step):
                b = branch_index(kind, g)
                layer = 0 if kind == "pre" else 1
                second = step.endswith("2")
                if step in ("sums", "sums2", "var", "var2", "norm", "norm2"):
                    n = norm_index(kind, g, int(second))
                if step in ("sums", "sums2"):
                    if second:
                        act.wait_ge(s["wkv_done"], b + 1)
                    else:
                        if b >= 1:
                            act.wait_ge(s["wkv_done"], b)
                        if kind == "pre":
                            act.wait_ge(x_in[g % 3], 16 * (g // 3 + 1))
                        else:
                            act.wait_ge(s["resid_done"], g + 1)
                    act.activation(SPs[:, :], xg(g), ACT.Square).then_inc(s["sq_done"], 1)
                elif step in ("var", "var2"):
                    if posts_before(b):
                        act.wait_ge(s["x3_out"], 16 * posts_before(b))
                    act.wait_ge(s["stat_done"], n + 1)
                    act.activation(M_, bank(S0), ACT.Copy)
                    act.activation(MSQ, bank(S0), ACT.Square).then_inc(s["msq_done"], 1)
                    act.wait_ge(s["var_done"], n + 1)
                    link(act.activation(RS, VAR, ACT.Ln, bias=eps[:, 0:1]))
                    act.activation(RS, RS, ACT.Exp, scale=-0.5).then_inc(s["r0_done"], 1)
                elif step == "norm2":
                    act.wait_ge(s["k_done"], n + 1)
                    if g >= 2:
                        act.wait_ge(s["b_done"], J * (g - 1))
                    act.activation(xs[:, g % 2, 0, :, :].rearrange("p c n -> p (c n)"), K[:, :], ACT.Copy).then_inc(s["xh_done"], 1)
                elif step == "exps":
                    n = norm_index(kind, g, 0)
                    act.wait_ge(s["k_done"], n + 1)
                    for c in range(C):
                        ins = act.activation(ch(E1, c), ch(K, c), ACT.Exp, bias=nm[:, layer, c:c + 1])
                    ins.then_inc(s["e1_done"], 1)
                    for c in range(C):
                        ins = act.activation(ch(E2, c), ch(K, c), ACT.Exp, bias=um[:, layer, c:c + 1])
                    ins.then_inc(s["e2_done"], 1)
                elif step == "mix":
                    act.wait_ge(s["den_done"], b + 1)
                    act.wait_ge(s["ev2_done"], b + 1)
                    link(act.activation(later(E2), later(K), ACT.Ln))
                    act.activation(later(E2), later(E2), ACT.Exp, scale=-1.0).then_inc(s["rec_done"], 1)
                elif step == "rows":
                    for i in range(TILES):
                        act.wait_ge(s["tr_done"], TILES * g + i + 1)
                        act.activation(E1[:, i * D:(i + 1) * D], bank(S0 + i % 2), ACT.Copy).then_inc(s["xt_done"], 1)
                elif step == "gate":
                    act.wait_ge(s["tvar_done"], g + 1)
                    link(act.activation(rt[:, 0, :], mv[:, :, 1], ACT.Ln, bias=eps[:, 0:1]))
                    act.activation(rt[:, 0, :], rt[:, 0, :], ACT.Exp, scale=-0.5).then_inc(s["tr0_done"], 1)
                    act.wait_ge(s["d_done"], g + 1)
                    act.activation(q[4][:, :, :], q[4][:, :, :], ACT.Exp, scale=-1.0)
                    act.activation(q[5][:, :, :], q[5][:, :, :], ACT.Exp, scale=-1.0).then_inc(s["ex_done"], 1)

            def chunk(g, j):
                n = J * g + j
                if n >= 2:
                    act.wait_ge(s["hid_done"], n - 1)
                act.wait_ge(s["a_done"], n + 1)
                link(act.activation(sg[:, j % 2, :], bank(ABANK), ACT.Exp, scale=-1.0 / (SW * SX)))
                link(act.activation(sg[:, j % 2, :], sg[:, j % 2, :], ACT.Ln, bias=one[:, 0:1]))
                act.activation(sg[:, j % 2, :], sg[:, j % 2, :], ACT.Exp, scale=-1.0).then_inc(s["sig_done"], 1)
                if n >= 2:
                    act.wait_ge(s["down_done"], n - 1)
                act.wait_ge(s["hid_done"], n + 1)
                act.activation(hs[:, j % 2, 0, :], hid[:, j % 2, :], ACT.Copy).then_inc(s["hh_done"], 1)

            for u in range(2):
                scale_unit(u)
                high_unit(u)
            run("pre", 0, "sums")
            run("pre", 0, "var")
            for u in range(2, 4):
                scale_unit(u)
                high_unit(u)
            run("pre", 0, "exps")
            run("pre", 0, "mix")
            run("pre", 0, "sums2")
            run("pre", 0, "var2")
            run("pre", 0, "norm2")
            for u in range(4, UNITS):
                scale_unit(u)
                high_unit(u)
            for jj in range(4):
                had_high(jj)
            for g in range(NG):
                for j in range(J):
                    chunk(g, j)
                    step = steps_beside(g, j)
                    if step:
                        run(*step)
            for step in POST_STEPS:
                run("post", NG - 1, step)

            h1 = PS[:, 0:2, :].rearrange("p b n -> p (b n)")

            def block(i, par):
                act.wait_ge(s["up_done"], i + 1)
                act.wait_ge(s["act_done"], i + 1)
                act.activation(sil[0], h1, ACT.Exp, scale=-1.0).then_inc(s["sig_steps"], 1)
                act.wait_ge(s["sig_steps"], 2 * i + 1)
                act.activation(sil[0], sil[0], ACT.Ln, bias=one[:, 0:1]).then_inc(s["sig_steps"], 1)
                act.wait_ge(s["sig_steps"], 2 * i + 2)
                act.activation(sil[0], sil[0], ACT.Exp, scale=-1.0).then_inc(s["sil_done"], 1)
                act.wait_ge(s["xT_done"], i + 2)
                act.activation(xTt[1 - par], bank(4).rearrange("p (c n) -> p c n", c=C), ACT.Copy).then_inc(s["xT_used"], 1)
                act.wait_ge(s["aT_done"], i + 1)
                if not (isinstance(i, int) and i == 0):
                    act.wait_ge(s["slot_down"], i)
                act.activation(aTt[par], aTp, ACT.Copy).then_inc(s["aT_used"], 1)

            aTp = PS[:, 5:7, :].rearrange("p b n -> p (b n)").rearrange("p (c n) -> p c n", c=IC)
            act.wait_ge(s["xn_out"], 16 * NG)
            act.wait_ge(s["xT_done"], 1)
            act.activation(xTt[0], bank(4).rearrange("p (c n) -> p c n", c=C), ACT.Copy).then_inc(s["xT_used"], 1)
            block(0, 0)
            with act.Fori(0, (SLOTS - 1) // 2, 1) as m:
                block(2 * m + 1, 1)
                block(2 * m + 2, 0)

        @blockv.vector
        def _(ve):
            chain = [0]

            def link(ins):
                chain[0] += 1
                ins.then_inc(s["vchain"], 1)
                ve.wait_ge(s["vchain"], chain[0])

            ve.memset(eps[:, :], EPS).then_inc(s["zeroed"], 1)
            ve.memset(one[:, :], 1.0).then_inc(s["zeroed"], 1)
            link(ve.memset(cum[:, :], 0.0))
            ve.wait_ge(s["hot_in"], 48)
            for lay in range(2):
                link(ve.tensor_scalar(nm[:, lay, :], vec[:, 1 + 2 * lay, :], 0.0, -1.0, MAXO, MUL))
                link(ve.tensor_tensor(um[:, lay, :], vec[:, 1 + 2 * lay, :], nm[:, lay, :], ADD))
            ve.wait_ge(s["gains_th"], 1)
            link(ve.tensor_scalar(sc[:, 0:2], gn[:, 0:2], -1.0, None, MUL))
            link(ve.tensor_scalar(sc[:, 2:3], gn[:, 2:3], 1.0 / (SW * SH), None, MUL))
            link(ve.tensor_copy(sc[:, 3:4], gn[:, 3:4]))
            ve.wait_ge(s["dec_ready"], 1)

            def newton(r, tmp, var, scale):
                link(ve.tensor_tensor(tmp, r, r, MUL))
                link(ve.scalar_tensor_tensor(tmp, var, EPS, tmp, ADD, MUL))
                link(ve.tensor_scalar(tmp, tmp, -0.5 * scale, 1.5 * scale, MUL, ADD))
                link(ve.tensor_tensor(tmp, tmp, r, MUL))

            def run(kind, g, step):
                b = branch_index(kind, g)
                layer = 0 if kind == "pre" else 1
                second = step.endswith("2")
                if step in ("sums", "sums2", "var", "var2", "norm", "norm2"):
                    n = norm_index(kind, g, int(second))
                if step in ("sums", "sums2"):
                    if kind == "pre" and not second:
                        ve.wait_ge(x_in[g % 3], 16 * (g // 3 + 1))
                    xv = xg(g)
                    link(ve.tensor_tensor(E2[:, 0:2 * NT], xv[:, 0:2 * NT], xv[:, 2 * NT:4 * NT], ADD))
                    link(ve.tensor_tensor(E2[:, 2 * NT:3 * NT], E2[:, 0:NT], E2[:, NT:2 * NT], ADD))
                    ve.wait_ge(s["sq_done"], n + 1)
                    link(ve.tensor_tensor(SPs[:, 0:2 * NT], SPs[:, 0:2 * NT], SPs[:, 2 * NT:4 * NT], ADD))
                    ve.tensor_tensor(E2[:, 3 * NT:4 * NT], SPs[:, 0:NT], SPs[:, NT:2 * NT], ADD).then_inc(s["sums_done"], 1)
                elif step in ("var", "var2"):
                    ve.wait_ge(s["msq_done"], n + 1)
                    ve.tensor_tensor(VAR, bank(S1), MSQ, SUB).then_inc(s["var_done"], 1)
                    if posts_before(b):
                        ve.wait_ge(s["xn_out"], 16 * posts_before(b))
                    link(ve.tensor_tensor(cn(K[:, :]), cn(xg(g)), wide(M_), SUB))
                elif step in ("norm", "norm2"):
                    ve.wait_ge(s["r0_done"], n + 1)
                    ve.wait_ge(s["var_done"], n + 1)
                    newton(RS, MSQ, VAR, SX if second else 1.0)
                    ve.tensor_tensor(cn(K[:, :]), cn(K[:, :]), wide(MSQ), MUL).then_inc(s["k_done"], 1)
                    if second:
                        ve.wait_ge(s["xh_done"], g + 1)
                        ve.wait_ge(s["k_done"], n + 1)
                        f = lambda half: xs[:, g % 2, half, :, :].rearrange("p c n -> p (c n)")
                        ve.tensor_tensor(f(1), K[:, :], f(0), SUB).then_inc(s["xs_ready"], 1)
                elif step == "exps":
                    def scan(dst, src, last):
                        for a in range(C * NB):
                            c = a // NB
                            t = slice(a * T, (a + 1) * T)
                            ins = ve.tensor_tensor_scan(dst[:, t], dec[:, layer, c:c + 1].to_broadcast([P, T]), src[:, t], 0.0, MUL, ADD)
                        last(ins)

                    ve.wait_ge(s["e1_done"], b + 1)
                    scan(SQs, E1, lambda ins: ins.then_inc(s["q_done"], 1))
                    ve.wait_ge(s["ev1_done"], b + 1)
                    scan(SPs, K, link)
                    ve.wait_ge(s["e2_done"], b + 1)
                    ve.wait_ge(s["q_done"], b + 1)
                    ve.tensor_tensor(later(K), later(E2), before(SQs), ADD).then_inc(s["den_done"], 1)
                elif step == "mix":
                    ve.wait_ge(s["ev2_done"], b + 1)
                    link(ve.tensor_tensor(later(E1), later(E1), before(SPs), ADD))
                    ve.wait_ge(s["rec_done"], b + 1)
                    ve.wait_ge(s["den_done"], b + 1)
                    link(ve.tensor_tensor(later(K), later(K), later(E2), MUL))
                    link(ve.scalar_tensor_tensor(later(K), later(K), -2.0, later(E2), ADD, MUL))
                    link(ve.tensor_tensor(later(E1), later(E1), later(K), MUL))
                    ve.tensor_scalar(seq(E1)[:, :, 0:1], seq(V)[:, :, 0:1], -1.0, None, MUL).then_inc(s["v_used"], 1)
                    ve.wait_ge(s["v_used"], b + 1)
                    ve.scalar_tensor_tensor(xg(g), E1[:, :], sc[:, layer:layer + 1], xg(g), MUL, ADD).then_inc(s["wkv_done"], 1)
                    ve.wait_ge(s["wkv_done"], b + 1)
                elif step == "rows":
                    ve.wait_ge(s["lg_done"], g + 1)
                    ve.tensor_copy(q[0][:, :, :], bank(S1)[:, 0:TILES * E].rearrange("p (i e) -> p i e", e=E)).then_inc(s["raw_done"], 1)
                    for i in range(TILES):
                        ve.wait_ge(s["xt_done"], TILES * g + i + 1)
                        link(ve.bn_stats(st[:, i, :], E1[:, i * D:(i + 1) * D]))
                        ins = ve.bn_aggr(mv[:, i, :], st[:, i, :])
                    ins.then_inc(s["tvar_done"], 1)
                    ve.wait_ge(s["tvar_done"], g + 1)
                elif step == "gate":
                    ve.wait_ge(s["tr0_done"], g + 1)
                    newton(rt[:, 0, :], rt[:, 1, :], mv[:, :, 1], 1.0)
                    for i in range(TILES):
                        ins = ve.tensor_scalar(K[:, i * D:(i + 1) * D], E1[:, i * D:(i + 1) * D], mv[:, i, 0:1], rt[:, 1, i:i + 1], SUB, MUL)
                    ins.then_inc(s["xn_done"], 1)
                    wide_e = lambda t: t.rearrange("p (i o) -> p i o", o=1).to_broadcast([P, TILES, E])
                    wide_i = lambda t: t.rearrange("p (o e) -> p o e", o=1).to_broadcast([P, TILES, E])
                    tt = lambda o, a, bb, op: link(ve.tensor_tensor(o, a, bb, op))
                    lg, oh1, oh2, ml, d1, d2, keep1, keep2, f, tmp = (t[:, :, :] for t in q)
                    mx1, mx2, w_, sm, _, _ = (t[:, :] for t in r4)
                    rs = rt[:, 1, :]
                    tt(lg, lg, wide_e(rs), MUL)

                    def top(src, mx, oh):
                        link(ve.tensor_reduce(mx, src, AX, MAXO))
                        tt(tmp, src, wide_e(mx), ALU.is_equal)
                        tt(tmp, tmp, wide_i(dsc[:, :]), MUL)
                        link(ve.tensor_reduce(w_, tmp, AX, MAXO))
                        tt(oh, wide_e(w_), wide_i(dsc[:, :]), ALU.is_equal)

                    ve.wait_ge(s["const_in"], 16 * len(CONSTS))
                    top(lg, mx1, oh1)
                    link(ve.scalar_tensor_tensor(ml, oh1, -3e38, lg, MUL, ADD))
                    top(ml, mx2, oh2)
                    tt(d1, wide_e(mx1), lg, SUB)
                    tt(d2, wide_e(mx2), ml, SUB)
                    link(ve.scalar_tensor_tensor(f, lg, -1.0, lg, MUL, MAXO))
                    tt(tmp, f, wide_e(mx1), MAXO)
                    link(ve.scalar_tensor_tensor(keep1, tmp, JITTER2, d1, MUL, ALU.is_ge))
                    tt(tmp, f, wide_e(mx2), MAXO)
                    link(ve.scalar_tensor_tensor(keep2, tmp, JITTER2, d2, MUL, ALU.is_ge))
                    ve.tensor_tensor(f, oh1, oh2, ADD).then_inc(s["d_done"], 1)
                    ve.wait_ge(s["d_done"], g + 1)
                    for i in range(TILES):
                        link(ve.tensor_copy(a16[:, 1, i, :], cum[:, :]))
                        tt(cum[:, :], cum[:, :], q[8][:, i, :], ADD)
                    ve.tensor_copy(a16[:, 0, :, :], f).then_inc(s["asg_done"], 1)
                    ve.wait_ge(s["ex_done"], g + 1)
                    for k, (d, keep) in enumerate(((d1, keep1), (d2, keep2))):
                        tt(d, d, keep, MUL)
                        link(ve.tensor_reduce(sm, d, AX, ADD))
                        link(ve.reciprocal(sm, sm))
                        link(ve.tensor_scalar(mult[:, k, g * TILES:(g + 1) * TILES], sm, sc[:, 3:4], None, MUL))
                elif step == "rank":
                    ve.wait_ge(s["rank_done"], g + 1)
                    rk = bank(S0)[:, 0:TILES * E].rearrange("p (i e) -> p i e", e=E)
                    wide_i = lambda t: t.rearrange("p (o e) -> p o e", o=1).to_broadcast([P, TILES, E])
                    _, oh1, oh2, _, _, _, _, _, f, tmp = (t[:, :, :] for t in q)
                    link(ve.tensor_tensor(f, rk, wide_i(ebs[:, :]), ADD))
                    for k, oh in enumerate((oh1, oh2)):
                        link(ve.tensor_tensor(tmp, oh, f, MUL))
                        link(ve.tensor_reduce(r4[3][:, :], tmp, AX, ADD))
                        ins = ve.tensor_copy(pos[:, k, g * TILES:(g + 1) * TILES], r4[3][:, :])
                        if k == 0:
                            link(ins)
                    ins.then_inc(s["pos_done"], 1)
                    ve.wait_ge(s["pos_done"], g + 1)

            def chunk(g, j):
                n = J * g + j
                ve.wait_ge(s["sig_done"], n + 1)
                ve.tensor_tensor(sg[:, j % 2, :], bank(ABANK), sg[:, j % 2, :], MUL).then_inc(s["s_done"], 1)
                ve.wait_ge(s["b_done"], n + 1)
                ve.wait_ge(s["s_done"], n + 1)
                ve.scalar_tensor_tensor(hid[:, j % 2, :], sg[:, j % 2, :], SH / (SW * SX) ** 2, bank(BBANK), MUL, MUL).then_inc(s["hid_done"], 1)
                ve.wait_ge(s["hh_done"], n + 1)
                ve.tensor_tensor(hs[:, j % 2, 1, :], hid[:, j % 2, :], hs[:, j % 2, 0, :], SUB).then_inc(s["hl_done"], 1)

            def resid(g):
                ve.wait_ge(s["down_done"], J * (g + 1))
                for c in range(C):
                    ins = ve.scalar_tensor_tensor(X[:, g % 3, c, :], bank(OUT0 + c), sc[:, 2:3], X[:, g % 3, c, :], MUL, ADD)
                ins.then_inc(s["resid_done"], 1)
                ve.wait_ge(s["resid_done"], g + 1)

            for step in PRE_STEPS:
                run("pre", 0, step)
            ve.wait_ge(s["const_in"], 16 * len(CONSTS))
            ve.tensor_reduce(gsum[:, :], gw[:, :, :].rearrange("p c e -> p e c"), AX, ADD).then_inc(s["gsum_ready"], 1)
            ve.wait_ge(s["gmean_ready"], 1)
            ve.wait_ge(s["gsum_ready"], 1)
            link(ve.tensor_copy(gsum[:, :], bank(S0)[:, 0:E]))
            ve.tensor_tensor(gw[:, :, :], gw[:, :, :], gsum[:, :].rearrange("p (o e) -> p o e", o=1).to_broadcast([P, C, E]), SUB).then_inc(s["gw_ready"], 1)
            for jj in range(4):
                ve.wait_ge(s["had_hi"], jj + 1)
                for a in range(4):
                    ins = ve.scalar_tensor_tensor(w2s[:, 1, 4 * a + jj, :], bank(OUT0 + a), float(H) ** -0.5, w2s[:, 0, 4 * a + jj, :], MUL, SUB)
                ins.then_inc(s["had_lo"], 1)
            for g in range(NG):
                if g >= 1:
                    resid(g - 1)
                for j in range(J):
                    chunk(g, j)
                    step = steps_beside(g, j)
                    if step:
                        run(*step)
            resid(NG - 1)
            for step in POST_STEPS:
                run("post", NG - 1, step)

            ve.tensor_copy(a16[:, 0, 0, :], cum[:, :]).then_inc(s["cum_done"], 1)
            ve.wait_ge(s["count_done"], 1)
            link(ve.tensor_copy(cnt[:, 0, :], bank(S1)[:, 0:E]))
            wide16 = cnt[:, 0, :].rearrange("p (e o) -> p e o", o=1).to_broadcast([P, E, 16])
            link(ve.tensor_tensor(cmp16[:, :, :], wide16, blk[:, :].rearrange("p (o j) -> p o j", o=1).to_broadcast([P, E, 16]), ALU.is_gt))
            link(ve.tensor_reduce(cnt[:, 1, :], cmp16[:, :, :], AX, ADD))
            link(ve.memset(cnt[:, 3, :], 1.0))
            link(ve.tensor_tensor_scan(cnt[:, 2, :], cnt[:, 3, :], cnt[:, 1, :], 0.0, MUL, ADD))
            link(ve.tensor_scalar(cnt[:, 4, :], cnt[:, 2, :], 1.0, None, ADD))
            link(ve.tensor_copy(starts[:, :], cnt[:, 4, :]))
            sno3 = sno[:, :].rearrange("p (s o) -> p s o", o=1).to_broadcast([P, SLOTS + 1, E])
            cum3 = cnt[:, 2, :].rearrange("p (o e) -> p o e", o=1).to_broadcast([P, SLOTS + 1, E])
            link(ve.tensor_tensor(sle[:, :, :], sno3, cum3, ALU.is_ge))
            link(ve.tensor_reduce(sl[:, 0, :], sle[:, :, :], AX, ADD))
            link(ve.tensor_tensor(sle[:, :, :], sle[:, :, :], cum3, MUL))
            link(ve.tensor_reduce(sl[:, 1, :], sle[:, :, :], AX, MAXO))
            link(ve.tensor_tensor(sl[:, 2, :], sno[:, :], sl[:, 1, :], SUB))
            link(ve.tensor_scalar(sl[:, 2, :], sl[:, 2, :], float(P), None, MUL))
            link(ve.scalar_tensor_tensor(sl[:, 2, :], sl[:, 0, :], float(TOK), sl[:, 2, :], MUL, ADD))
            link(ve.tensor_copy(table[:, 2, :], sl[:, 2, :]))
            link(ve.tensor_scalar(sl[:, 0, :], sl[:, 0, :], float(E - 1), None, ALU.min))
            link(ve.tensor_copy(table[:, 0, :], sl[:, 0, :]))
            link(ve.tensor_scalar(sl[:, 3, :], sl[:, 0, :], 1.0, 32.0, ADD, MUL))
            link(ve.tensor_copy(table[:, 3, :], sl[:, 3, :]))
            link(ve.tensor_scalar(sl[:, 1, :], sl[:, 0, :], 1.0, None, ALU.is_equal))
            for e in range(3, E, 2):
                link(ve.scalar_tensor_tensor(sl[:, 1, :], sl[:, 0, :], float(e), sl[:, 1, :], ALU.is_equal, ADD))
            link(ve.tensor_scalar(sl[:, 1, :], sl[:, 1, :], float(EXPERT), None, MUL))
            link(ve.memset(cnt[:, 5, 0:1], 0.0))
            link(ve.tensor_scalar(cnt[:, 5, 1:E], cnt[:, 1, 0:E - 1], float(P), -float(TOK), MUL, ADD))
            link(ve.tensor_copy(posf[:, :, E], pos[:, :, :].rearrange("p k i -> p (k i)")))
            n2 = 2 * TOK // P
            link(ve.tensor_tensor(posf[:, :, 0:E], posf[:, :, E:E + 1].to_broadcast([P, n2, E]),
                                  ebs[:, :].rearrange("p (o e) -> p o e", o=1).to_broadcast([P, n2, E]), ALU.is_ge))
            link(ve.tensor_tensor(posf[:, :, 0:E], posf[:, :, 0:E],
                                  cnt[:, 5, :].rearrange("p (o e) -> p o e", o=1).to_broadcast([P, n2, E]), MUL))
            link(ve.tensor_reduce(cmp16[:, :, :].rearrange("p e j -> p (e j)")[:, 0:n2], posf[:, :, :], AX, ADD))
            link(ve.tensor_copy(ypos[:, :, :].rearrange("p k i -> p (k i)"), cmp16[:, :, :].rearrange("p e j -> p (e j)")[:, 0:n2]))
            ve.tensor_copy(table[:, 1, :], sl[:, 1, :]).then_inc(s["table_done"], 1)

            h1 = PS[:, 0:2, :].rearrange("p b n -> p (b n)")
            h3 = PS[:, 2:4, :].rearrange("p b n -> p (b n)")

            def hidden(i):
                ve.wait_ge(s["sil_done"], i + 1)
                ve.tensor_tensor(sil[0], sil[0], h1, MUL).then_inc(s["g1_done"], 1)
                ve.wait_ge(s["g1_done"], i + 1)
                if not (isinstance(i, int) and i == 0):
                    ve.wait_ge(s["aT_done"], i)
                ve.tensor_tensor(sil[1], sil[0], h3, MUL).then_inc(s["act_done"], 1)

            def evac_y(i, par):
                ve.wait_ge(s["slot_down"], i + 2)
                ve.tensor_copy(yt[par], bank(7)).then_inc(s["y_ready"], 1)

            ve.memset(cnt[:, 5, 0:1], 0.0).then_inc(s["act_done"], 1)
            ve.memset(cnt[:, 5, 1:2], 0.0).then_inc(s["y_ready"], 1)
            hidden(0)
            hidden(1)
            evac_y(0, 0)
            hidden(2)
            evac_y(1, 1)
            with ve.Fori(1, (SLOTS - 1) // 2, 1) as m:
                hidden(2 * m + 1)
                ve.wait_ge(ysto[0], 16 * m)
                evac_y(2 * m, 0)
                hidden(2 * m + 2)
                ve.wait_ge(ysto[1], 16 * m)
                evac_y(2 * m + 1, 1)
            ve.wait_ge(ysto[0], 16 * ((SLOTS - 1) // 2))
            evac_y(SLOTS - 1, 0)
            for i in range(TOK // P):
                ve.wait_ge(c_x3[i % 2], 16 * (i // 2 + 1))
                ve.wait_ge(c_y[i % 2], 32 * (i // 2 + 1))
                link(ve.scalar_tensor_tensor(cx3[i % 2], cy[i % 2][0], mult[:, 0, i:i + 1], cx3[i % 2], MUL, ADD))
                ve.scalar_tensor_tensor(cx3[i % 2], cy[i % 2][1], mult[:, 1, i:i + 1], cx3[i % 2], MUL, ADD).then_inc(s["c_out"], 1)

        @blockv.tensor
        def _(te):
            PAIRS = ((0, 0), (0, 1), (1, 0))

            def run(kind, g, step):
                b = branch_index(kind, g)
                second = step.endswith("2")
                if step in ("sums", "sums2"):
                    n = norm_index(kind, g, int(second))
                    te.wait_ge(s["sums_done"], n + 1)
                    if n >= 1:
                        te.wait_ge(s["var_done"], n)
                    te.matmul(bank(S0), onesm[:, :], E2[:, 2 * NT:3 * NT], start=True, stop=True)
                    te.matmul(bank(S1), onesm[:, :], E2[:, 3 * NT:4 * NT], start=True, stop=True).then_inc(s["stat_done"], 1)
                elif step == "rows":
                    te.wait_ge(s["wkv_done"], b + 1)
                    te.wait_ge(s["gw_ready"], 1)
                    xv = X[:, g % 3, :, :]
                    for i in range(TILES):
                        for c in range(C):
                            ins = te.matmul(bank(S1)[:, i * E:(i + 1) * E], xv[:, c, i * P:(i + 1) * P], gw[:, c, :], start=(c == 0), stop=(c == C - 1))
                    ins.then_inc(s["lg_done"], 1)
                    for i in range(TILES):
                        if i == 1:
                            te.wait_ge(s["raw_done"], g + 1)
                        if i >= 2:
                            te.wait_ge(s["xt_done"], TILES * g + i - 1)
                        for c in range(C):
                            ins = te.transpose(bank(S0 + i % 2)[:, c * P:(c + 1) * P], xv[:, c, i * P:(i + 1) * P], idn[:, :])
                        ins.then_inc(s["tr_done"], 1)
                elif step == "rank":
                    te.wait_ge(s["asg_done"], g + 1)
                    te.wait_ge(s["xt_done"], TILES * (g + 1))
                    for i in range(TILES):
                        o = bank(S0)[:, i * E:(i + 1) * E]
                        te.matmul(o, tris[:, :], a16[:, 0, i, :], start=True, stop=False)
                        ins = te.matmul(o, ones1[:, :], a16[:, 1, i, :], start=False, stop=True)
                    ins.then_inc(s["rank_done"], 1)

            def up(g, j):
                for bk, w, sem_, free in ((ABANK, w1s, "a_done", "s_done"), (BBANK, w3s, "b_done", "hid_done")):
                    if not (isinstance(j, int) and J * g + j == 0):
                        te.wait_ge(s[free], J * g + j)
                    for n, (a, b) in enumerate(PAIRS):
                        for c in range(C):
                            ins = te.matmul(bank(bk), w[:, a, c, bass.ds(j * P, P)], xs[:, g % 2, b, c, :],
                                            start=(n == 0 and c == 0), stop=(n == 2 and c == C - 1))
                    ins.then_inc(s[sem_], 1)

            def down(g, j, par):
                te.wait_ge(s["hl_done"], J * g + j + 1)
                first, last = isinstance(j, int) and j == 0, isinstance(j, int) and j == J - 1
                if first and g >= 1:
                    te.wait_ge(s["resid_done"], g)
                for c in range(C):
                    for n, (a, b) in enumerate(PAIRS):
                        ins = te.matmul(bank(OUT0 + c), w2s[:, a, j, c * P:(c + 1) * P], hs[:, par, b, :],
                                        start=first and n == 0, stop=last and n == 2)
                ins.then_inc(s["down_done"], 1)
                return ins

            te.wait_ge(s["hot_in"], 48)
            run("pre", 0, "sums")
            run("pre", 0, "sums2")
            te.wait_ge(s["gsum_ready"], 1)
            te.wait_ge(s["var_done"], 2)
            te.matmul(bank(S0)[:, 0:E], onesm[:, :], gsum[:, :], start=True, stop=True).then_inc(s["gmean_ready"], 1)
            te.wait_ge(s["const_in"], 16 * len(CONSTS))
            te.wait_ge(s["stage_lo"], UNITS)
            for jj in range(4):
                if jj >= 1:
                    te.wait_ge(s["had_lo"], jj)
                for a in range(4):
                    for n, (k, half) in enumerate((k, half) for k in range(4) for half in range(2)):
                        sign = bin(a & k).count("1") % 2
                        ins = te.matmul(bank(OUT0 + a), hads[:, sign, :], w2s[:, half, 4 * k + jj, :], start=(n == 0), stop=(n == 7))
                ins.then_inc(s["had_out"], 1)
            te.wait_ge(s["had_lo"], 4)
            te.wait_ge(s["gw_ready"], 1)
            for g in range(NG):
                te.wait_ge(s["xs_ready"], g + 1)
                up(g, 0)
                for j in range(1, J):
                    up(g, j)
                    down(g, j - 1, (j - 1) % 2)
                    step = steps_beside(g, j - 1)
                    if step:
                        run(*step)
                down(g, J - 1, (J - 1) % 2)
                step = steps_beside(g, J - 1)
                if step:
                    run(*step)
            for step in POST_STEPS:
                run("post", NG - 1, step)
            te.wait_ge(s["cum_done"], 1)
            te.matmul(bank(S1)[:, 0:E], ones1[:, :], a16[:, 0, 0, :], start=True, stop=True).then_inc(s["count_done"], 1)

            te.wait_ge(s["table_done"], 1)
            load = lambda row, i, top: te.value_load(table[0:1, row, bass.ds(i, 1)], min_val=0, max_val=top)

            def rows_t(i, n, par):
                te.wait_ge(row_s[par], 16 * n)
                if not (isinstance(i, int) and i == 0):
                    te.wait_ge(s["xT_used"], i)
                for c in range(C):
                    ins = te.transpose(bank(4)[:, c * P:(c + 1) * P], grow[par][:, c * P:(c + 1) * P], idn[:, :])
                    if isinstance(i, int) and i == 0 and c == 0:
                        ins.then_inc(s["slot_down"], 1)
                ins.then_inc(s["xT_done"], 1)

            def experts_up(i, par):
                loads, off = load(3, i, 32 * E), load(1, i, EXPERT)
                te.wait_ge(wl, loads)
                te.wait_ge(s["xT_used"], i + 1)
                te.wait_ge(s["act_done"], i + 1)
                for c in range(C):
                    for n in range(2 * I // NT):
                        ins = te.matmul(bank(n), xTt[par][:, c, :], weights[:, bass.ds(off + (2 * c * I + n * NT), NT)],
                                        start=(c == 0), stop=(c == C - 1))
                ins.then_inc(s["up_done"], 1)

            def experts_down(i, par):
                off = load(1, i, EXPERT)
                te.wait_ge(s["aT_used"], i + 1)
                te.wait_ge(s["y_ready"], i + 1)
                for c in range(IC):
                    ins = te.matmul(bank(7), aTt[par][:, c, :], weights[:, bass.ds(off + (2 * C * I + c * D), D)],
                                    start=(c == 0), stop=(c == IC - 1))
                ins.then_inc(s["slot_down"], 1)

            def hidden_t(i):
                te.wait_ge(s["act_done"], i + 2)
                if not (isinstance(i, int) and i == 0):
                    te.wait_ge(s["aT_used"], i)
                for c in range(IC):
                    ins = te.transpose(bank(5 + c // C)[:, c % C * P:(c % C + 1) * P], sil[1][:, c * P:(c + 1) * P], idn[:, :])
                ins.then_inc(s["aT_done"], 1)

            def block(i, n, par):
                experts_up(i, par)
                rows_t(i + 1, n, 1 - par)
                if not (isinstance(i, int) and i == 0):
                    experts_down(i - 1, 1 - par)
                hidden_t(i)

            rows_t(0, 1, 0)
            block(0, 1, 0)
            with te.Fori(0, (SLOTS - 1) // 2, 1) as m:
                block(2 * m + 1, m + 2, 1)
                block(2 * m + 2, m + 2, 0)
            experts_down(SLOTS - 1, 0)


def kernel(**inputs):
    import numpy as np
    import concourse.bacc as bacc
    from concourse.bass_utils import run_bass_kernel_spmd as launch

    a = {k: np.asarray(v) for k, v in inputs.items()}

    def channel_major(v):
        return v.reshape(NG, NB, T, C, P).transpose(0, 4, 3, 1, 2).reshape(NG, P, W)

    def cols(v):
        return v.reshape(C, P).T

    def rows_first(w, chunks):
        return w.T.reshape(chunks, P, w.shape[0]).transpose(1, 0, 2)

    h = np.array([[1.0]], np.float32)
    while h.shape[0] < P:
        h = np.block([[h, h], [h, -h]])
    lower = np.arange(P)
    wide = lambda v, dt: np.broadcast_to(np.asarray(v, dt), (P, len(v)))
    w1 = a["L1_ffn_w1"].transpose(0, 2, 1).reshape(E, C, P, I)
    w3 = a["L1_ffn_w3"].transpose(0, 2, 1).reshape(E, C, P, I)
    arrays = {
        "x_cm": channel_major(a["x"]),
        "ctx_cm": channel_major(a["ctx_2048"]),
        "vecs": np.stack([cols(a[n]) for n in ("L0_xattn_w", "L0_xattn_u", "L1_xattn_time_decay", "L1_xattn_time_first")], 1),
        "gains": np.broadcast_to(np.concatenate([a["g_xattn"], a["g_ffn"]]), (P, 4)),
        "w1t": rows_first(a["L0_ffn_W1"], C),
        "w3t": rows_first(a["L0_ffn_W3"], C),
        "w2t": rows_first(a["L0_ffn_W2"], J),
        "gate_t": rows_first(a["L1_ffn_gate_w"], C),
        "e13": np.concatenate([w1, w3], 3).transpose(0, 2, 1, 3).reshape(E, P, 2 * C * I),
        "e2": a["L1_ffn_w2"].transpose(0, 2, 1).reshape(E, IC, P, D).transpose(0, 2, 1, 3).reshape(E, P, IC * D),
        "had": np.stack([h, -h], 1).astype(np.float16),
        "ones_mean": np.full((P, P), 1.0 / D, np.float32),
        "ident": np.eye(P, dtype=np.float32),
        "tri": (lower[:, None] < lower[None, :]).astype(np.float16),
        "ones16": np.ones((P, P), np.float16),
        "tok_id": (lower[:, None] + P * np.arange(TOK // P)[None, :]).astype(np.int32),
        "ebase": wide(TOK * np.arange(E), np.float32),
        "desc": wide(E - np.arange(E), np.float32),
        "blocks": wide(P * np.arange(16), np.float32),
        "slot_no": wide(np.arange(SLOTS + 1), np.float32),
    }
    arrays = {k: np.ascontiguousarray(v) for k, v in arrays.items()}
    nc = bacc.Bacc("TRN2", target_bir_lowering=False, num_devices=1)
    args = [nc.dram_tensor(n, v.shape, mybir.dt.from_np(v.dtype), kind="ExternalInput").ap() for n, v in arrays.items()]
    out = nc.dram_tensor("out", (TOK, D), F32, kind="ExternalOutput").ap()
    build(nc, *args, out)
    r = launch(nc, [arrays], core_ids=[0])
    return r.results[0]["out"].reshape(BATCH, T, D)
```

```python
from contextlib import ExitStack

import concourse.bass as bass
from concourse import mybir

F32 = mybir.dt.float32
F16 = mybir.dt.float16
I32 = mybir.dt.int32
ALU = mybir.AluOpType
ACT = mybir.ActivationFunctionType
AX = mybir.AxisListType.X

P = 128
BATCH, T, D = 8, 256, 512
TOK = BATCH * T
NT = 512
NG = TOK // NT
NB = NT // T
C = D // P
W = C * NT
H = 2048
J = H // P
E, I = 8, 1024
IC = I // P
TILES = NT // P
EPS = 1e-5
JITTER2 = 0.02

SW = 256.0
SX = 64.0
SH = 16.0

SLOTS = 2 * TOK // P + E - 1
SPARE = (SLOTS - 2 * TOK // P) * P
LIST = E * TOK + SPARE + P
EXPERT = 2 * C * I + IC * D
ADD, SUB, MUL, MAXO = ALU.add, ALU.subtract, ALU.mult, ALU.max

BRANCHES = [("pre", 0)]
for _g in range(NG):
    if _g + 1 < NG:
        BRANCHES.append(("pre", _g + 1))
    if _g >= 1:
        BRANCHES.append(("post", _g - 1))
BRANCHES.append(("post", NG - 1))
NORMS = [(k, g, i) for k, g in BRANCHES for i in range(2 if k == "pre" else 1)]

BESIDE = [[("pre", 1, "sums")], [("pre", 1, "norm")], [("pre", 1, "exps"), ("post", -2, "rank")], [("pre", 1, "scan")],
          [("pre", 1, "den")], [("pre", 1, "mix")], [("pre", 1, "sums2")], [("pre", 1, "norm2")],
          [("pre", 1, "low"), ("post", -1, "sums")], [("post", -1, "norm")], [("post", -1, "exps")],
          [("post", -1, "scan")], [("post", -1, "den")], [("post", -1, "mix")], [("post", -1, "rows")],
          [("post", -1, "gate")]]
PROLOGUE = ["sums", ("w", 0), "norm", ("q", 0), ("w", 1), "exps", ("q", 1), ("w", 2), "scan", ("w", 3), ("q", 2), "den",
            ("w", 4), "mix", ("q", 3), ("w", 5), "sums2", ("w", 6), "norm2", ("w", 7), "low"]
EPILOGUE = [("post", NG - 1, s) for s in ("sums", "norm", "exps")] + [("post", NG - 2, "rank")] + \
           [("post", NG - 1, s) for s in ("scan", "den", "mix", "rows", "gate", "rank")]


def branch_index(kind, g):
    return BRANCHES.index((kind, g))


def norm_index(kind, g, i):
    return NORMS.index((kind, g, i))


def steps_beside(g, j):
    return [(kind, g + d, step) for kind, d, step in BESIDE[j] if 0 <= g + d < NG]


def build(nc, x_cm, ctx_cm, vecs, gains, w1t, w3t, w2t, gate_t, e13, e2, had, ones_mean, ident,
          tri, ones16, tok_id, ebase, desc, blocks, slot_no, spare_rows, zero_rows, out):
    ctx = ExitStack()
    with ctx:
        def sb(name, shape, dt):
            return ctx.enter_context(nc.sbuf_tensor(name, shape, dt))

        def sem(name):
            return ctx.enter_context(nc.semaphore(name))

        xn_rows = nc.dram_tensor("xn_rows", (TOK + P, D), F32).ap()
        row_list = nc.dram_tensor("row_list", (LIST, 2), I32).ap()

        weights = sb("weights", [P, 2 * EXPERT], F32)
        w16 = weights[:, :].bitcast(F16)
        n1 = 2 * C * H
        w1s = w16[:, 0:n1].rearrange("p (s c h) -> p s c h", s=2, c=C)
        w3s = w16[:, n1:2 * n1].rearrange("p (s c h) -> p s c h", s=2, c=C)
        w2s = w16[:, 2 * n1:2 * n1 + 2 * J * D].rearrange("p (s j d) -> p s j d", s=2, j=J)
        X = sb("X", [P, 3, C, NT], F32)
        V = sb("V", [P, W], F32)
        K = sb("K", [P, W], F32)
        E1 = sb("E1", [P, W], F32)
        E2 = sb("E2", [P, W], F32)
        SPs = sb("SPs", [P, W], F32)
        SQs = sb("SQs", [P, W], F32)
        xs = sb("xs", [P, 2, 2, C, NT], F16)
        work = sb("work", [P, 4 * NT], F32)
        sg = work[:, 0:2 * NT].rearrange("p (a n) -> p a n", a=2)
        hid = work[:, 2 * NT:4 * NT].rearrange("p (a n) -> p a n", a=2)
        hs = sb("hs", [P, 2, 2, NT], F16)
        vec = sb("vec", [P, 4, C], F32)
        dec = sb("dec", [P, 2, C], F32)
        nm = sb("nm", [P, 2, C], F32)
        um = sb("um", [P, 2, C], F32)
        gn = sb("gn", [P, 4], F32)
        sc = sb("sc", [P, 4], F32)
        eps = sb("eps", [P, 1], F32)
        one = sb("one", [P, 1], F32)
        hads = sb("hads", [P, 2, P], F16)
        onesm = sb("onesm", [P, P], F32)
        idn = sb("idn", [P, P], F32)
        tris = sb("tris", [P, P], F16)
        ones1 = sb("ones1", [P, P], F16)
        gw = sb("gw", [P, C, E], F32)
        gsum = sb("gsum", [P, E], F32)
        entry = sb("entry", [P, 2, TOK // P, 2], I32)
        ebs = sb("ebs", [P, E], F32)
        dsc = sb("dsc", [P, E], F32)
        blk = sb("blk", [P, 16], F32)
        sno = sb("sno", [P, SLOTS + 1], F32)
        st = sb("st", [P, TILES, 6], F32)
        mv = sb("mv", [P, TILES, 2], F32)
        rt = sb("rt", [P, 4, TILES], F32)
        q = [sb(f"q{n}", [P, TILES, E], F32) for n in range(10)]
        r4 = [sb(f"r4_{n}", [P, TILES], F32) for n in range(6)]
        a16 = sb("a16", [P, 2, TILES, E], F16)
        cum = sb("cum", [P, E], F32)
        pos = sb("pos", [P, 2, TOK // P], I32)
        cnt = sb("cnt", [P, 6, E], F32)
        cmp16 = sb("cmp16", [P, E, 16], F32)
        sl = sb("sl", [P, 4, SLOTS + 1], F32)
        sle = sb("sle", [P, SLOTS + 1, E], F32)
        table = sb("table", [P, 4, SLOTS + 1], I32)
        idxt = sb("idxt", [P, 2, 2], I32)
        outl = sb("outl", [P, 2, 2], I32)
        starts = sb("starts", [P, E], I32)

        PS = ctx.enter_context(nc.psum_tensor("PS", [P, 8, NT], F32))
        bank = lambda n: PS[:, n, :]
        ABANK, BBANK, OUT0, S0, S1 = 0, 1, 2, 6, 7

        names = """const_in hot_in gains_th scal_ready decay_a dec_ready gsum_ready gmean_ready gw_ready zeroed
            w_in w_hi w_lo q_bf q_hi q_lo xsum_done had_out had_hi had_lo spare_in
            v_in v_used sq_done sums_done stat_done msq_done var_done r0_done k_done xh_done xs_ready
            e1_done e2_done ev1_done ev2_done q_done den_done rec_done wkv_done
            a_done b_done sig_done s_done hid_done hh_done hl_done down_done out_done resid_done
            lg_done tr_done xt_done raw_done tvar_done tr0_done xn_done x3_out xn_out d_done ex_done
            asg_done rank_done pos_done scat_done cum_done count_done table_done
            idx_in rows_in xT_done xT_used up_done act_done slot_down aT_done aT_used y_out
            y_ready gathers g1_done sil_done sig_steps vchain achain gchain""".split()
        s = {n: sem(n) for n in names}
        x_in = [sem(f"x_in{n}") for n in range(3)]
        q_in = [sem(f"q_in{n}") for n in range(2)]
        wl = sem("expert_in")
        idx_s = [sem(f"idx_in{n}") for n in range(2)]
        row_s = [sem(f"rows_in{n}") for n in range(2)]
        ysto = [sem(f"y_store{n}") for n in range(2)]
        out_s = [sem(f"out_in{n}") for n in range(2)]

        entry_w = entry[:, :, :, :].bitcast(F32)
        outl_w = outl[:, :, :].bitcast(F32)
        xg = lambda g: X[:, g % 3, :, :].rearrange("p c n -> p (c n)")
        ch = lambda t, c: t[:, c * NT:(c + 1) * NT]
        seq = lambda t: t[:, :].rearrange("p (a t) -> p a t", t=T)
        later = lambda t: seq(t)[:, :, 1:T]
        before = lambda t: seq(t)[:, :, 0:T - 1]
        wide = lambda t: t.rearrange("p (o n) -> p o n", o=1).to_broadcast([P, C, NT])
        cn = lambda t: t.rearrange("p (c n) -> p c n", c=C)
        M_, MSQ, VAR, RS = (E1[:, n * NT:(n + 1) * NT] for n in range(4))
        wstage = work[:, :]
        qstage = [X[:, 1 + n, :, :].rearrange("p c n -> p (c n)") for n in range(2)]
        qtmp = xs[:, 1, :, :, :].rearrange("p a c n -> p (a c n)").bitcast(F32)
        NW, NQ = 2 * C, 4

        def w_dst(u, half):
            return (w1s, w3s)[u // C][:, half, u % C, :]

        def q_dst(u, half):
            return w2s[:, half, 4 * u:4 * u + 4, :].rearrange("p j d -> p (j d)")

        blockv = ctx.enter_context(nc.Block())
        CONSTS = [(hads[:, :, :], had), (idn[:, :], ident), (tris[:, :], tri), (ones1[:, :], ones16),
                  (entry[:, :, :, :], tok_id), (ebs[:, :], ebase), (dsc[:, :], desc), (blk[:, :], blocks),
                  (sno[:, :], slot_no), (gw[:, :, :], gate_t)]
        posts_before = lambda b: sum(kind == "post" for kind, _ in BRANCHES[:b])

        grow = [SPs[:, n * D:(n + 1) * D] for n in range(2)]
        xTt = [SPs[:, (2 + n) * D:(3 + n) * D].rearrange("p (c n) -> p c n", c=C) for n in range(2)]
        sil = [K[:, 0:I], K[:, I:2 * I]]
        aTt = [SQs[:, n * I:(n + 1) * I].rearrange("p (c n) -> p c n", c=IC) for n in range(2)]
        yt = [V[:, n * D:(n + 1) * D] for n in range(2)]

        @blockv.sync
        def _(sp):
            def load_v(b):
                if b >= 1:
                    sp.wait_ge(s["v_used"], b)
                sp.dma_start(V[:, :], ctx_cm[BRANCHES[b][1], :, :]).then_inc(s["v_in"], 16)

            def load_x(g):
                if g in (1, 2):
                    sp.wait_ge(s["q_lo"], NQ)
                if g >= 3:
                    sp.wait_ge(s["tr_done"], TILES * (g - 2))
                sp.dma_start(xg(g), x_cm[g, :, :]).then_inc(x_in[g % 3], 16)

            sp.dma_start(vec[:, :, :], vecs).then_inc(s["hot_in"], 16)
            sp.dma_start(gn[:, :], gains).then_inc(s["hot_in"], 16)
            sp.dma_start(onesm[:, :], ones_mean).then_inc(s["hot_in"], 16)
            load_x(0)
            load_v(0)
            def load_w(u):
                if u >= 1:
                    sp.wait_ge(s["w_lo"], u)
                sp.dma_start(wstage, (w1t, w3t)[u // C][:, u % C, :]).then_inc(s["w_in"], 16)

            def load_q(u):
                if u >= 2:
                    sp.wait_ge(s["q_lo"], u - 1)
                sp.dma_start(qstage[u % 2], w2t[:, 4 * u:4 * u + 4, :].rearrange("p j d -> p (j d)")).then_inc(q_in[u % 2], 16)

            load_w(0)
            load_q(0)
            load_q(1)
            for t, a in CONSTS:
                sp.dma_start(t, a).then_inc(s["const_in"], 16)
            for item in [x for x in PROLOGUE if isinstance(x, tuple)]:
                if item[0] == "w" and item[1] + 1 < NW:
                    load_w(item[1] + 1)
                if item[0] == "q" and item[1] + 2 < NQ:
                    load_q(item[1] + 2)
            sp.dma_start(row_list.rearrange("(p n) o -> p (n o)", p=P), spare_rows).then_inc(s["spare_in"], 16)
            sp.dma_start(xn_rows[TOK:TOK + P, :], zero_rows).then_inc(s["spare_in"], 16)
            sp.dma_start(out[TOK:TOK + P, :], zero_rows).then_inc(s["spare_in"], 16)
            load_x(1)
            for b in range(1, len(BRANCHES)):
                load_v(b)
                kind, g = BRANCHES[b]
                if kind == "pre" and g + 1 < 3:
                    load_x(g + 1)
                if kind == "post":
                    sp.wait_ge(s["xt_done"], TILES * (g + 1))
                    sp.dma_start(out[g * NT:(g + 1) * NT, :].rearrange("(i p) d -> p i d", p=P), cn(E1[:, :])).then_inc(s["x3_out"], 16)
                    if g + 3 < NG:
                        load_x(g + 3)
                    sp.wait_ge(s["xn_done"], g + 1)
                    sp.dma_start(xn_rows[g * NT:(g + 1) * NT, :].rearrange("(i p) d -> p i d", p=P), cn(K[:, :])).then_inc(s["xn_out"], 16)
            sp.wait_ge(s["down_done"], NG * J)
            wreg = weights[:, :].rearrange("p (b n) -> p b n", b=2)
            sp.wait_ge(s["table_done"], 1)
            for e in range(E):
                if e >= 1:
                    sp.wait_ge(wl, 32 * e)
                if e >= 2:
                    first = sp.value_load(starts[0:1, e - 2:e - 1], min_val=1, max_val=SLOTS + 1)
                    sp.wait_ge(s["slot_down"], first)
                sp.dma_start(wreg[:, e % 2, 0:2 * C * I], e13[e, :, :]).then_inc(wl, 16)
                sp.dma_start(wreg[:, e % 2, 2 * C * I:EXPERT], e2[e, :, :]).then_inc(wl, 16)

        @blockv.gpsimd
        def _(gp):
            chain = [0]

            def link(ins):
                chain[0] += 1
                ins.then_inc(s["gchain"], 1)
                gp.wait_ge(s["gchain"], chain[0])

            def butterflies(u):
                a = qstage[u % 2]
                gp.wait_ge(q_in[u % 2], 16 * (u // 2 + 1))
                b4 = qtmp.rearrange("p (b a d) -> p b a d", b=2, a=2)
                a4 = a.rearrange("p (b a d) -> p b a d", b=2, a=2)
                link(gp.tensor_tensor(b4[:, :, 0, :], a4[:, :, 0, :], a4[:, :, 1, :], ADD))
                link(gp.tensor_tensor(b4[:, :, 1, :], a4[:, :, 0, :], a4[:, :, 1, :], SUB))
                link(gp.tensor_tensor(a[:, 0:2 * D], qtmp[:, 0:2 * D], qtmp[:, 2 * D:4 * D], ADD))
                gp.tensor_tensor(a[:, 2 * D:4 * D], qtmp[:, 0:2 * D], qtmp[:, 2 * D:4 * D], SUB).then_inc(s["q_bf"], 1)
                gp.wait_ge(s["q_bf"], u + 1)

            def xsum(kind, g, second):
                b, n = branch_index(kind, g), norm_index(kind, g, int(second))
                if b + second:
                    gp.wait_ge(s["wkv_done"], b + second)
                if n >= 1:
                    gp.wait_ge(s["stat_done"], n)
                    gp.wait_ge(s["xsum_done"], n)
                if kind == "pre" and not second:
                    gp.wait_ge(x_in[g % 3], 16 * (g // 3 + 1))
                if kind == "post":
                    gp.wait_ge(s["resid_done"], g + 1)
                xv = xg(g)
                link(gp.tensor_tensor(E2[:, 0:2 * NT], xv[:, 0:2 * NT], xv[:, 2 * NT:4 * NT], ADD))
                gp.tensor_tensor(E2[:, 2 * NT:3 * NT], E2[:, 0:NT], E2[:, NT:2 * NT], ADD).then_inc(s["xsum_done"], 1)

            def products(b):
                gp.wait_ge(s["v_in"], 16 * (b + 1))
                gp.wait_ge(s["e1_done"], b + 1)
                gp.wait_ge(s["e2_done"], b + 1)
                gp.tensor_tensor(K[:, :], E1[:, :], V[:, :], MUL).then_inc(s["ev1_done"], 1)
                gp.wait_ge(s["q_done"], b + 1)
                gp.wait_ge(s["ev1_done"], b + 1)
                gp.tensor_tensor(E1[:, :], E2[:, :], V[:, :], MUL).then_inc(s["ev2_done"], 1)

            def scatter(g):
                gp.wait_ge(s["spare_in"], 48)
                gp.wait_ge(s["pos_done"], g + 1)
                gp.wait_ge(s["const_in"], 16 * len(CONSTS))
                for i in range(g * TILES, (g + 1) * TILES):
                    for k in range(2):
                        gp.indirect_dma_start(row_list, bass.IndirectOffsetOnAxis(ap=pos[:, k, i:i + 1], axis=0),
                                              entry[:, k, i, :], None).then_inc(s["scat_done"], 16)

            def run(kind, g, step):
                if step in ("sums", "sums2"):
                    xsum(kind, g, step == "sums2")
                if step == "exps":
                    products(branch_index(kind, g))
                if step == "rank":
                    scatter(g)

            run("pre", 0, "sums")
            butterflies(0)
            butterflies(1)
            run("pre", 0, "exps")
            butterflies(2)
            butterflies(3)
            run("pre", 0, "sums2")
            for g in range(NG):
                for j in range(J):
                    for step in steps_beside(g, j):
                        run(*step)
            for step in EPILOGUE:
                run(*step)

            gp.wait_ge(s["table_done"], 1)
            gp.wait_ge(s["scat_done"], 16 * 2 * TOK // P)
            gp.wait_ge(s["xn_out"], 16 * NG)
            gp.wait_ge(s["wkv_done"], len(BRANCHES))

            def first_row(i):
                return gp.value_load(table[0:1, 2, bass.ds(i, 1)], min_val=0, max_val=LIST - P)

            def load_list(i, n, par):
                gp.dma_start(idxt[:, par, :], row_list[bass.ds(first_row(i), P), :]).then_inc(idx_s[par], 16)

            def load_out_list(i, par):
                gp.dma_start(outl[:, par, :], row_list[bass.ds(first_row(i), P), :]).then_inc(out_s[par], 16)

            def gather(i, n, par):
                gp.wait_ge(idx_s[par], 16 * n)
                gp.sem_inc(s["gathers"], 1)
                gp.indirect_dma_start(grow[par], None, xn_rows, bass.IndirectOffsetOnAxis(ap=idxt[:, par, 0:1], axis=0)).then_inc(row_s[par], 16)

            def add_out(i, n, par, last=False):
                if not (isinstance(i, int) and i == 0):
                    gp.wait_ge(ysto[1 - par], 16 * (n - 1 + par))
                    gp.sem_inc(s["gathers"], 1)
                if not last:
                    load_out_list(i + 1, 1 - par)
                gp.wait_ge(s["y_ready"], i + 2)
                gp.sem_inc(s["gathers"], 1)
                gp.indirect_dma_start(out, bass.IndirectOffsetOnAxis(ap=outl[:, par, 0:1], axis=0), yt[par], None, compute_op=ADD).then_inc(ysto[par], 16)

            gp.wait_ge(s["x3_out"], 16 * NG)
            load_list(0, 1, 0)
            load_list(1, 1, 1)
            load_out_list(0, 0)
            gather(0, 1, 0)
            gather(1, 1, 1)

            def block(i, n, par):
                gp.wait_ge(row_s[par], 16 * n)
                gp.sem_inc(s["gathers"], 1)
                load_list(i + 2, n + 1, par)
                gp.wait_ge(s["xT_done"], i + 1)
                gather(i + 2, n + 1, par)
                add_out(i, n, par)

            block(0, 1, 0)
            block(1, 1, 1)
            with gp.Fori(1, (SLOTS - 1) // 2, 1) as m:
                block(2 * m, m + 1, 0)
                block(2 * m + 1, m + 1, 1)
            n = (SLOTS - 1) // 2
            add_out(2 * n, n + 1, 0, last=True)
            gp.wait_ge(row_s[0], 16 * (n + 1))
            gp.wait_ge(row_s[1], 16 * (n + 1))
            for k in range(2):
                gp.wait_ge(ysto[k], 16 * (n + 1 - k))

        @blockv.scalar
        def _(act):
            chain = [0]

            def link(ins):
                chain[0] += 1
                ins.then_inc(s["achain"], 1)
                act.wait_ge(s["achain"], chain[0])

            act.wait_ge(s["hot_in"], 48)
            act.activation(gn[:, :], gn[:, :], ACT.Tanh).then_inc(s["gains_th"], 1)
            act.preload_act_table_set("natural_log_exp_and_others")
            act.wait_ge(s["zeroed"], 2)
            link(act.activation(vec[:, 2, :], vec[:, 2, :], ACT.Exp))
            act.activation(dec[:, 0, :], vec[:, 0, :], ACT.Exp)
            act.activation(dec[:, 1, :], vec[:, 2, :], ACT.Exp, scale=-1.0).then_inc(s["dec_ready"], 1)

            def w_high(u):
                act.wait_ge(s["w_in"], 16 * (u + 1))
                act.activation(w_dst(u, 0), wstage, ACT.Copy, scale=SW).then_inc(s["w_hi"], 1)

            def q_high(u):
                act.wait_ge(s["q_bf"], u + 1)
                act.activation(q_dst(u, 0), qstage[u % 2], ACT.Copy, scale=SW).then_inc(s["q_hi"], 1)

            def had_high(jj):
                act.wait_ge(s["had_out"], jj + 1)
                for a in range(4):
                    ins = act.activation(w2s[:, 0, 4 * a + jj, :], bank(OUT0 + a), ACT.Copy, scale=float(H) ** -0.5)
                ins.then_inc(s["had_hi"], 1)

            def run(kind, g, step):
                b = branch_index(kind, g)
                layer = 0 if kind == "pre" else 1
                second = step.endswith("2")
                if step in ("sums", "sums2", "norm", "norm2"):
                    n = norm_index(kind, g, int(second))
                if step in ("sums", "sums2"):
                    if second:
                        act.wait_ge(s["wkv_done"], b + 1)
                    else:
                        if b >= 1:
                            act.wait_ge(s["wkv_done"], b)
                        if kind == "pre":
                            act.wait_ge(x_in[g % 3], 16 * (g // 3 + 1))
                        else:
                            act.wait_ge(s["resid_done"], g + 1)
                    act.activation(SPs[:, :], xg(g), ACT.Square).then_inc(s["sq_done"], 1)
                elif step in ("norm", "norm2"):
                    if posts_before(b):
                        act.wait_ge(s["x3_out"], 16 * posts_before(b))
                    act.wait_ge(s["stat_done"], n + 1)
                    act.activation(M_, bank(S0), ACT.Copy)
                    act.activation(MSQ, bank(S0), ACT.Square).then_inc(s["msq_done"], 1)
                    act.wait_ge(s["var_done"], n + 1)
                    link(act.activation(RS, VAR, ACT.Ln, bias=eps[:, 0:1]))
                    act.activation(RS, RS, ACT.Exp, scale=-0.5).then_inc(s["r0_done"], 1)
                elif step == "low":
                    act.wait_ge(s["k_done"], norm_index(kind, g, 1) + 1)
                    if g >= 2:
                        act.wait_ge(s["b_done"], J * (g - 1))
                    act.activation(xs[:, g % 2, 0, :, :].rearrange("p c n -> p (c n)"), K[:, :], ACT.Copy).then_inc(s["xh_done"], 1)
                elif step == "exps":
                    n = norm_index(kind, g, 0)
                    act.wait_ge(s["k_done"], n + 1)
                    for c in range(C):
                        ins = act.activation(ch(E1, c), ch(K, c), ACT.Exp, bias=nm[:, layer, c:c + 1])
                    ins.then_inc(s["e1_done"], 1)
                    for c in range(C):
                        ins = act.activation(ch(E2, c), ch(K, c), ACT.Exp, bias=um[:, layer, c:c + 1])
                    ins.then_inc(s["e2_done"], 1)
                elif step == "den":
                    act.wait_ge(s["den_done"], b + 1)
                    act.wait_ge(s["ev2_done"], b + 1)
                    link(act.activation(later(E2), later(K), ACT.Ln))
                    act.activation(later(E2), later(E2), ACT.Exp, scale=-1.0).then_inc(s["rec_done"], 1)
                elif step == "rows":
                    for i in range(TILES):
                        act.wait_ge(s["tr_done"], TILES * g + i + 1)
                        act.activation(E1[:, i * D:(i + 1) * D], bank(S0 + i % 2), ACT.Copy).then_inc(s["xt_done"], 1)
                elif step == "gate":
                    act.wait_ge(s["tvar_done"], g + 1)
                    link(act.activation(rt[:, 0, :], mv[:, :, 1], ACT.Ln, bias=eps[:, 0:1]))
                    act.activation(rt[:, 0, :], rt[:, 0, :], ACT.Exp, scale=-0.5).then_inc(s["tr0_done"], 1)
                    act.wait_ge(s["d_done"], g + 1)
                    act.activation(q[4][:, :, :], q[4][:, :, :], ACT.Exp, scale=-1.0)
                    act.activation(q[5][:, :, :], q[5][:, :, :], ACT.Exp, scale=-1.0).then_inc(s["ex_done"], 1)

            def chunk(g, j):
                n = J * g + j
                if n >= 2:
                    act.wait_ge(s["hid_done"], n - 1)
                act.wait_ge(s["a_done"], n + 1)
                link(act.activation(sg[:, j % 2, :], bank(ABANK), ACT.Exp, scale=-1.0 / (SW * SX)))
                link(act.activation(sg[:, j % 2, :], sg[:, j % 2, :], ACT.Ln, bias=one[:, 0:1]))
                act.activation(sg[:, j % 2, :], sg[:, j % 2, :], ACT.Exp, scale=-1.0).then_inc(s["sig_done"], 1)
                if n >= 2:
                    act.wait_ge(s["down_done"], n - 1)
                act.wait_ge(s["hid_done"], n + 1)
                act.activation(hs[:, j % 2, 0, :], hid[:, j % 2, :], ACT.Copy).then_inc(s["hh_done"], 1)

            for item in PROLOGUE:
                if isinstance(item, str):
                    run("pre", 0, item)
                else:
                    (w_high if item[0] == "w" else q_high)(item[1])
            for jj in range(4):
                had_high(jj)
            for g in range(NG):
                for j in range(J):
                    chunk(g, j)
                    for step in steps_beside(g, j):
                        run(*step)
            for step in EPILOGUE:
                run(*step)

            h1 = PS[:, 0:2, :].rearrange("p b n -> p (b n)")

            def block(i, par):
                act.wait_ge(s["up_done"], i + 1)
                act.wait_ge(s["act_done"], i + 1)
                act.activation(sil[0], h1, ACT.Exp, scale=-1.0).then_inc(s["sig_steps"], 1)
                act.wait_ge(s["sig_steps"], 2 * i + 1)
                act.activation(sil[0], sil[0], ACT.Ln, bias=one[:, 0:1]).then_inc(s["sig_steps"], 1)
                act.wait_ge(s["sig_steps"], 2 * i + 2)
                act.activation(sil[0], sil[0], ACT.Exp, scale=-1.0).then_inc(s["sil_done"], 1)
                act.wait_ge(s["xT_done"], i + 2)
                act.activation(xTt[1 - par], bank(4).rearrange("p (c n) -> p c n", c=C), ACT.Copy).then_inc(s["xT_used"], 1)
                act.wait_ge(s["aT_done"], i + 1)
                if not (isinstance(i, int) and i == 0):
                    act.wait_ge(s["slot_down"], i)
                act.activation(aTt[par], aTp, ACT.Copy).then_inc(s["aT_used"], 1)

            aTp = PS[:, 5:7, :].rearrange("p b n -> p (b n)").rearrange("p (c n) -> p c n", c=IC)
            act.wait_ge(s["xn_out"], 16 * NG)
            act.wait_ge(s["xT_done"], 1)
            act.activation(xTt[0], bank(4).rearrange("p (c n) -> p c n", c=C), ACT.Copy).then_inc(s["xT_used"], 1)
            block(0, 0)
            with act.Fori(0, (SLOTS - 1) // 2, 1) as m:
                block(2 * m + 1, 1)
                block(2 * m + 2, 0)

        @blockv.vector
        def _(ve):
            chain = [0]

            def link(ins):
                chain[0] += 1
                ins.then_inc(s["vchain"], 1)
                ve.wait_ge(s["vchain"], chain[0])

            ve.memset(eps[:, :], EPS).then_inc(s["zeroed"], 1)
            ve.memset(one[:, :], 1.0).then_inc(s["zeroed"], 1)
            link(ve.memset(cum[:, :], 0.0))
            ve.wait_ge(s["hot_in"], 48)
            for lay in range(2):
                link(ve.tensor_scalar(nm[:, lay, :], vec[:, 1 + 2 * lay, :], 0.0, -1.0, MAXO, MUL))
                link(ve.tensor_tensor(um[:, lay, :], vec[:, 1 + 2 * lay, :], nm[:, lay, :], ADD))
            ve.wait_ge(s["gains_th"], 1)
            link(ve.tensor_scalar(sc[:, 0:2], gn[:, 0:2], -1.0, None, MUL))
            link(ve.tensor_scalar(sc[:, 2:3], gn[:, 2:3], 1.0 / (SW * SH), None, MUL))
            link(ve.tensor_copy(sc[:, 3:4], gn[:, 3:4]))
            ve.wait_ge(s["dec_ready"], 1)

            def newton(r, tmp, var, scale):
                link(ve.tensor_tensor(tmp, r, r, MUL))
                link(ve.scalar_tensor_tensor(tmp, var, EPS, tmp, ADD, MUL))
                link(ve.tensor_scalar(tmp, tmp, -0.5 * scale, 1.5 * scale, MUL, ADD))
                link(ve.tensor_tensor(tmp, tmp, r, MUL))

            def run(kind, g, step):
                b = branch_index(kind, g)
                layer = 0 if kind == "pre" else 1
                second = step.endswith("2")
                if step in ("sums", "sums2", "norm", "norm2"):
                    n = norm_index(kind, g, int(second))
                if step in ("sums", "sums2"):
                    ve.wait_ge(s["sq_done"], n + 1)
                    link(ve.tensor_tensor(SPs[:, 0:2 * NT], SPs[:, 0:2 * NT], SPs[:, 2 * NT:4 * NT], ADD))
                    ve.tensor_tensor(E2[:, 3 * NT:4 * NT], SPs[:, 0:NT], SPs[:, NT:2 * NT], ADD).then_inc(s["sums_done"], 1)
                elif step in ("norm", "norm2"):
                    ve.wait_ge(s["msq_done"], n + 1)
                    ve.tensor_tensor(VAR, bank(S1), MSQ, SUB).then_inc(s["var_done"], 1)
                    if posts_before(b):
                        ve.wait_ge(s["xn_out"], 16 * posts_before(b))
                    link(ve.tensor_tensor(cn(K[:, :]), cn(xg(g)), wide(M_), SUB))
                    if kind == "pre" and not second:
                        ve.wait_ge(x_in[g % 3], 16 * (g // 3 + 1))
                    ve.wait_ge(s["r0_done"], n + 1)
                    ve.wait_ge(s["var_done"], n + 1)
                    newton(RS, MSQ, VAR, SX if second else 1.0)
                    ve.tensor_tensor(cn(K[:, :]), cn(K[:, :]), wide(MSQ), MUL).then_inc(s["k_done"], 1)
                elif step == "low":
                    ve.wait_ge(s["xh_done"], g + 1)
                    ve.wait_ge(s["k_done"], norm_index(kind, g, 1) + 1)
                    f = lambda half: xs[:, g % 2, half, :, :].rearrange("p c n -> p (c n)")
                    ve.tensor_tensor(f(1), K[:, :], f(0), SUB).then_inc(s["xs_ready"], 1)
                elif step == "scan":
                    def scan(dst, src, last):
                        for a in range(C * NB):
                            c = a // NB
                            t = slice(a * T, (a + 1) * T)
                            ins = ve.tensor_tensor_scan(dst[:, t], dec[:, layer, c:c + 1].to_broadcast([P, T]), src[:, t], 0.0, MUL, ADD)
                        last(ins)

                    ve.wait_ge(s["e1_done"], b + 1)
                    scan(SQs, E1, lambda ins: ins.then_inc(s["q_done"], 1))
                    ve.wait_ge(s["ev1_done"], b + 1)
                    scan(SPs, K, link)
                elif step == "den":
                    ve.wait_ge(s["e2_done"], b + 1)
                    ve.wait_ge(s["q_done"], b + 1)
                    ve.tensor_tensor(later(K), later(E2), before(SQs), ADD).then_inc(s["den_done"], 1)
                    ve.wait_ge(s["ev2_done"], b + 1)
                    link(ve.tensor_tensor(later(E1), later(E1), before(SPs), ADD))
                elif step == "mix":
                    ve.wait_ge(s["rec_done"], b + 1)
                    ve.wait_ge(s["den_done"], b + 1)
                    link(ve.tensor_tensor(later(K), later(K), later(E2), MUL))
                    link(ve.scalar_tensor_tensor(later(K), later(K), -2.0, later(E2), ADD, MUL))
                    link(ve.tensor_tensor(later(E1), later(E1), later(K), MUL))
                    ve.tensor_scalar(seq(E1)[:, :, 0:1], seq(V)[:, :, 0:1], -1.0, None, MUL).then_inc(s["v_used"], 1)
                    ve.wait_ge(s["v_used"], b + 1)
                    ve.scalar_tensor_tensor(xg(g), E1[:, :], sc[:, layer:layer + 1], xg(g), MUL, ADD).then_inc(s["wkv_done"], 1)
                    ve.wait_ge(s["wkv_done"], b + 1)
                elif step == "rows":
                    ve.wait_ge(s["lg_done"], g + 1)
                    ve.tensor_copy(q[0][:, :, :], bank(S1)[:, 0:TILES * E].rearrange("p (i e) -> p i e", e=E)).then_inc(s["raw_done"], 1)
                    for i in range(TILES):
                        ve.wait_ge(s["xt_done"], TILES * g + i + 1)
                        link(ve.bn_stats(st[:, i, :], E1[:, i * D:(i + 1) * D]))
                        ins = ve.bn_aggr(mv[:, i, :], st[:, i, :])
                    ins.then_inc(s["tvar_done"], 1)
                    ve.wait_ge(s["tvar_done"], g + 1)
                elif step == "gate":
                    ve.wait_ge(s["tr0_done"], g + 1)
                    newton(rt[:, 0, :], rt[:, 1, :], mv[:, :, 1], 1.0)
                    for i in range(TILES):
                        ins = ve.tensor_scalar(K[:, i * D:(i + 1) * D], E1[:, i * D:(i + 1) * D], mv[:, i, 0:1], rt[:, 1, i:i + 1], SUB, MUL)
                    ins.then_inc(s["xn_done"], 1)
                    wide_e = lambda t: t.rearrange("p (i o) -> p i o", o=1).to_broadcast([P, TILES, E])
                    wide_i = lambda t: t.rearrange("p (o e) -> p o e", o=1).to_broadcast([P, TILES, E])
                    tt = lambda o, a, bb, op: link(ve.tensor_tensor(o, a, bb, op))
                    lg, oh1, oh2, ml, d1, d2, keep1, keep2, f, tmp = (t[:, :, :] for t in q)
                    mx1, mx2, w_, sm, _, _ = (t[:, :] for t in r4)
                    rs = rt[:, 1, :]
                    tt(lg, lg, wide_e(rs), MUL)

                    def top(src, mx, oh):
                        link(ve.tensor_reduce(mx, src, AX, MAXO))
                        tt(tmp, src, wide_e(mx), ALU.is_equal)
                        tt(tmp, tmp, wide_i(dsc[:, :]), MUL)
                        link(ve.tensor_reduce(w_, tmp, AX, MAXO))
                        tt(oh, wide_e(w_), wide_i(dsc[:, :]), ALU.is_equal)

                    ve.wait_ge(s["const_in"], 16 * len(CONSTS))
                    top(lg, mx1, oh1)
                    link(ve.scalar_tensor_tensor(ml, oh1, -3e38, lg, MUL, ADD))
                    top(ml, mx2, oh2)
                    tt(d1, wide_e(mx1), lg, SUB)
                    tt(d2, wide_e(mx2), ml, SUB)
                    link(ve.scalar_tensor_tensor(f, lg, -1.0, lg, MUL, MAXO))
                    tt(tmp, f, wide_e(mx1), MAXO)
                    link(ve.scalar_tensor_tensor(keep1, tmp, JITTER2, d1, MUL, ALU.is_ge))
                    tt(tmp, f, wide_e(mx2), MAXO)
                    link(ve.scalar_tensor_tensor(keep2, tmp, JITTER2, d2, MUL, ALU.is_ge))
                    ve.tensor_tensor(f, oh1, oh2, ADD).then_inc(s["d_done"], 1)
                    ve.wait_ge(s["d_done"], g + 1)
                    for i in range(TILES):
                        link(ve.tensor_copy(a16[:, 1, i, :], cum[:, :]))
                        tt(cum[:, :], cum[:, :], q[8][:, i, :], ADD)
                    ve.tensor_copy(a16[:, 0, :, :], f).then_inc(s["asg_done"], 1)
                    ve.wait_ge(s["ex_done"], g + 1)
                    for k, (d, keep) in enumerate(((d1, keep1), (d2, keep2))):
                        tt(d, d, keep, MUL)
                        link(ve.tensor_reduce(sm, d, AX, ADD))
                        link(ve.reciprocal(sm, sm))
                        link(ve.tensor_scalar(entry_w[:, k, g * TILES:(g + 1) * TILES, 1], sm, sc[:, 3:4], None, MUL))
                elif step == "rank":
                    ve.wait_ge(s["rank_done"], g + 1)
                    rk = bank(S0)[:, 0:TILES * E].rearrange("p (i e) -> p i e", e=E)
                    wide_i = lambda t: t.rearrange("p (o e) -> p o e", o=1).to_broadcast([P, TILES, E])
                    _, oh1, oh2, _, _, _, _, _, f, tmp = (t[:, :, :] for t in q)
                    link(ve.tensor_tensor(f, rk, wide_i(ebs[:, :]), ADD))
                    for k, oh in enumerate((oh1, oh2)):
                        link(ve.tensor_tensor(tmp, oh, f, MUL))
                        link(ve.tensor_reduce(r4[3][:, :], tmp, AX, ADD))
                        ins = ve.tensor_copy(pos[:, k, g * TILES:(g + 1) * TILES], r4[3][:, :])
                        if k == 0:
                            link(ins)
                    ins.then_inc(s["pos_done"], 1)
                    ve.wait_ge(s["pos_done"], g + 1)

            def chunk(g, j):
                n = J * g + j
                ve.wait_ge(s["sig_done"], n + 1)
                ve.tensor_tensor(sg[:, j % 2, :], bank(ABANK), sg[:, j % 2, :], MUL).then_inc(s["s_done"], 1)
                ve.wait_ge(s["b_done"], n + 1)
                ve.wait_ge(s["s_done"], n + 1)
                ve.scalar_tensor_tensor(hid[:, j % 2, :], sg[:, j % 2, :], SH / (SW * SX) ** 2, bank(BBANK), MUL, MUL).then_inc(s["hid_done"], 1)
                ve.wait_ge(s["hh_done"], n + 1)
                ve.tensor_tensor(hs[:, j % 2, 1, :], hid[:, j % 2, :], hs[:, j % 2, 0, :], SUB).then_inc(s["hl_done"], 1)

            def resid(g):
                ve.wait_ge(s["down_done"], J * (g + 1))
                for c in range(C):
                    ins = ve.scalar_tensor_tensor(X[:, g % 3, c, :], bank(OUT0 + c), sc[:, 2:3], X[:, g % 3, c, :], MUL, ADD)
                ins.then_inc(s["resid_done"], 1)
                ve.wait_ge(s["resid_done"], g + 1)

            for item in PROLOGUE:
                if isinstance(item, str):
                    run("pre", 0, item)
                elif item[0] == "w":
                    ve.wait_ge(s["w_hi"], item[1] + 1)
                    ve.scalar_tensor_tensor(w_dst(item[1], 1), wstage, SW, w_dst(item[1], 0), MUL, SUB).then_inc(s["w_lo"], 1)
                else:
                    ve.wait_ge(s["q_hi"], item[1] + 1)
                    ve.scalar_tensor_tensor(q_dst(item[1], 1), qstage[item[1] % 2], SW, q_dst(item[1], 0), MUL, SUB).then_inc(s["q_lo"], 1)
            ve.wait_ge(s["const_in"], 16 * len(CONSTS))
            ve.tensor_reduce(gsum[:, :], gw[:, :, :].rearrange("p c e -> p e c"), AX, ADD).then_inc(s["gsum_ready"], 1)
            ve.wait_ge(s["gmean_ready"], 1)
            ve.wait_ge(s["gsum_ready"], 1)
            link(ve.tensor_copy(gsum[:, :], bank(S0)[:, 0:E]))
            ve.tensor_tensor(gw[:, :, :], gw[:, :, :], gsum[:, :].rearrange("p (o e) -> p o e", o=1).to_broadcast([P, C, E]), SUB).then_inc(s["gw_ready"], 1)
            for jj in range(4):
                ve.wait_ge(s["had_hi"], jj + 1)
                for a in range(4):
                    ins = ve.scalar_tensor_tensor(w2s[:, 1, 4 * a + jj, :], bank(OUT0 + a), float(H) ** -0.5, w2s[:, 0, 4 * a + jj, :], MUL, SUB)
                ins.then_inc(s["had_lo"], 1)
            for g in range(NG):
                if g >= 1:
                    resid(g - 1)
                for j in range(J):
                    chunk(g, j)
                    for step in steps_beside(g, j):
                        run(*step)
            resid(NG - 1)
            for step in EPILOGUE:
                run(*step)

            ve.tensor_copy(a16[:, 0, 0, :], cum[:, :]).then_inc(s["cum_done"], 1)
            ve.wait_ge(s["count_done"], 1)
            link(ve.tensor_copy(cnt[:, 0, :], bank(S1)[:, 0:E]))
            wide16 = cnt[:, 0, :].rearrange("p (e o) -> p e o", o=1).to_broadcast([P, E, 16])
            link(ve.tensor_tensor(cmp16[:, :, :], wide16, blk[:, :].rearrange("p (o j) -> p o j", o=1).to_broadcast([P, E, 16]), ALU.is_gt))
            link(ve.tensor_reduce(cnt[:, 1, :], cmp16[:, :, :], AX, ADD))
            link(ve.memset(cnt[:, 3, :], 1.0))
            link(ve.tensor_tensor_scan(cnt[:, 2, :], cnt[:, 3, :], cnt[:, 1, :], 0.0, MUL, ADD))
            link(ve.tensor_scalar(cnt[:, 4, :], cnt[:, 2, :], 1.0, None, ADD))
            link(ve.tensor_copy(starts[:, :], cnt[:, 4, :]))
            sno3 = sno[:, :].rearrange("p (s o) -> p s o", o=1).to_broadcast([P, SLOTS + 1, E])
            cum3 = cnt[:, 2, :].rearrange("p (o e) -> p o e", o=1).to_broadcast([P, SLOTS + 1, E])
            link(ve.tensor_tensor(sle[:, :, :], sno3, cum3, ALU.is_ge))
            link(ve.tensor_reduce(sl[:, 0, :], sle[:, :, :], AX, ADD))
            link(ve.tensor_tensor(sle[:, :, :], sle[:, :, :], cum3, MUL))
            link(ve.tensor_reduce(sl[:, 1, :], sle[:, :, :], AX, MAXO))
            link(ve.tensor_tensor(sl[:, 2, :], sno[:, :], sl[:, 1, :], SUB))
            link(ve.tensor_scalar(sl[:, 2, :], sl[:, 2, :], float(P), None, MUL))
            link(ve.scalar_tensor_tensor(sl[:, 2, :], sl[:, 0, :], float(TOK), sl[:, 2, :], MUL, ADD))
            link(ve.tensor_copy(table[:, 2, :], sl[:, 2, :]))
            link(ve.tensor_scalar(sl[:, 0, :], sl[:, 0, :], float(E - 1), None, ALU.min))
            link(ve.tensor_copy(table[:, 0, :], sl[:, 0, :]))
            link(ve.tensor_scalar(sl[:, 3, :], sl[:, 0, :], 1.0, 32.0, ADD, MUL))
            link(ve.tensor_copy(table[:, 3, :], sl[:, 3, :]))
            link(ve.tensor_scalar(sl[:, 1, :], sl[:, 0, :], 1.0, None, ALU.is_equal))
            for e in range(3, E, 2):
                link(ve.scalar_tensor_tensor(sl[:, 1, :], sl[:, 0, :], float(e), sl[:, 1, :], ALU.is_equal, ADD))
            link(ve.tensor_scalar(sl[:, 1, :], sl[:, 1, :], float(EXPERT), None, MUL))
            ve.tensor_copy(table[:, 1, :], sl[:, 1, :]).then_inc(s["table_done"], 1)

            h1 = PS[:, 0:2, :].rearrange("p b n -> p (b n)")
            h3 = PS[:, 2:4, :].rearrange("p b n -> p (b n)")

            def hidden(i):
                ve.wait_ge(s["sil_done"], i + 1)
                ve.tensor_tensor(sil[0], sil[0], h1, MUL).then_inc(s["g1_done"], 1)
                ve.wait_ge(s["g1_done"], i + 1)
                if not (isinstance(i, int) and i == 0):
                    ve.wait_ge(s["aT_done"], i)
                ve.tensor_tensor(sil[1], sil[0], h3, MUL).then_inc(s["act_done"], 1)

            def evac_y(i, n, par):
                ve.wait_ge(s["slot_down"], i + 2)
                ve.wait_ge(out_s[par], 16 * n)
                ve.tensor_scalar(yt[par], bank(7), outl_w[:, par, 1:2], None, MUL).then_inc(s["y_ready"], 1)

            ve.memset(cnt[:, 5, 0:1], 0.0).then_inc(s["act_done"], 1)
            ve.memset(cnt[:, 5, 1:2], 0.0).then_inc(s["y_ready"], 1)
            hidden(0)
            hidden(1)
            evac_y(0, 1, 0)
            hidden(2)
            evac_y(1, 1, 1)
            with ve.Fori(1, (SLOTS - 1) // 2, 1) as m:
                hidden(2 * m + 1)
                ve.wait_ge(ysto[0], 16 * m)
                evac_y(2 * m, m + 1, 0)
                hidden(2 * m + 2)
                ve.wait_ge(ysto[1], 16 * m)
                evac_y(2 * m + 1, m + 1, 1)
            ve.wait_ge(ysto[0], 16 * ((SLOTS - 1) // 2))
            evac_y(SLOTS - 1, (SLOTS + 1) // 2, 0)
        @blockv.tensor
        def _(te):
            PAIRS = ((0, 0), (0, 1), (1, 0))

            def run(kind, g, step):
                b = branch_index(kind, g)
                second = step.endswith("2")
                if step in ("sums", "sums2"):
                    n = norm_index(kind, g, int(second))
                    te.wait_ge(s["sums_done"], n + 1)
                    te.wait_ge(s["xsum_done"], n + 1)
                    if n >= 1:
                        te.wait_ge(s["var_done"], n)
                    norms_taken[0] = n + 1
                    te.matmul(bank(S0), onesm[:, :], E2[:, 2 * NT:3 * NT], start=True, stop=True)
                    te.matmul(bank(S1), onesm[:, :], E2[:, 3 * NT:4 * NT], start=True, stop=True).then_inc(s["stat_done"], 1)
                elif step == "rows":
                    te.wait_ge(s["wkv_done"], b + 1)
                    te.wait_ge(s["gw_ready"], 1)
                    xv = X[:, g % 3, :, :]
                    for i in range(TILES):
                        for c in range(C):
                            ins = te.matmul(bank(S1)[:, i * E:(i + 1) * E], xv[:, c, i * P:(i + 1) * P], gw[:, c, :], start=(c == 0), stop=(c == C - 1))
                    ins.then_inc(s["lg_done"], 1)
                    for i in range(TILES):
                        if i == 1:
                            te.wait_ge(s["raw_done"], g + 1)
                        if i >= 2:
                            te.wait_ge(s["xt_done"], TILES * g + i - 1)
                        for c in range(C):
                            ins = te.transpose(bank(S0 + i % 2)[:, c * P:(c + 1) * P], xv[:, c, i * P:(i + 1) * P], idn[:, :])
                        ins.then_inc(s["tr_done"], 1)
                elif step == "rank":
                    te.wait_ge(s["asg_done"], g + 1)
                    te.wait_ge(s["var_done"], norms_taken[0])
                    te.wait_ge(s["xt_done"], TILES * (g + 1))
                    for i in range(TILES):
                        o = bank(S0)[:, i * E:(i + 1) * E]
                        te.matmul(o, tris[:, :], a16[:, 0, i, :], start=True, stop=False)
                        ins = te.matmul(o, ones1[:, :], a16[:, 1, i, :], start=False, stop=True)
                    ins.then_inc(s["rank_done"], 1)

            norms_taken = [0]

            def up(g, j):
                for bk, w, sem_, free in ((ABANK, w1s, "a_done", "s_done"), (BBANK, w3s, "b_done", "hid_done")):
                    if not (isinstance(j, int) and J * g + j == 0):
                        te.wait_ge(s[free], J * g + j)
                    for n, (a, b) in enumerate(PAIRS):
                        for c in range(C):
                            ins = te.matmul(bank(bk), w[:, a, c, bass.ds(j * P, P)], xs[:, g % 2, b, c, :],
                                            start=(n == 0 and c == 0), stop=(n == 2 and c == C - 1))
                    ins.then_inc(s[sem_], 1)

            def down(g, j, par):
                te.wait_ge(s["hl_done"], J * g + j + 1)
                first, last = isinstance(j, int) and j == 0, isinstance(j, int) and j == J - 1
                if first and g >= 1:
                    te.wait_ge(s["resid_done"], g)
                for c in range(C):
                    for n, (a, b) in enumerate(PAIRS):
                        ins = te.matmul(bank(OUT0 + c), w2s[:, a, j, c * P:(c + 1) * P], hs[:, par, b, :],
                                        start=first and n == 0, stop=last and n == 2)
                ins.then_inc(s["down_done"], 1)
                return ins

            te.wait_ge(s["hot_in"], 48)
            run("pre", 0, "sums")
            run("pre", 0, "sums2")
            te.wait_ge(s["gsum_ready"], 1)
            te.wait_ge(s["var_done"], 2)
            te.matmul(bank(S0)[:, 0:E], onesm[:, :], gsum[:, :], start=True, stop=True).then_inc(s["gmean_ready"], 1)
            te.wait_ge(s["const_in"], 16 * len(CONSTS))
            te.wait_ge(s["q_lo"], NQ)
            for jj in range(4):
                if jj >= 1:
                    te.wait_ge(s["had_lo"], jj)
                for a in range(4):
                    for n, (k, half) in enumerate((k, half) for k in range(4) for half in range(2)):
                        sign = bin(a & k).count("1") % 2
                        ins = te.matmul(bank(OUT0 + a), hads[:, sign, :], w2s[:, half, 4 * k + jj, :], start=(n == 0), stop=(n == 7))
                ins.then_inc(s["had_out"], 1)
            te.wait_ge(s["had_lo"], 4)
            te.wait_ge(s["w_lo"], NW)
            te.wait_ge(s["gw_ready"], 1)
            for g in range(NG):
                te.wait_ge(s["xs_ready"], g + 1)
                up(g, 0)
                for j in range(1, J):
                    up(g, j)
                    down(g, j - 1, (j - 1) % 2)
                    for step in steps_beside(g, j - 1):
                        run(*step)
                down(g, J - 1, (J - 1) % 2)
                for step in steps_beside(g, J - 1):
                    run(*step)
            for step in EPILOGUE:
                run(*step)
            te.wait_ge(s["cum_done"], 1)
            te.matmul(bank(S1)[:, 0:E], ones1[:, :], a16[:, 0, 0, :], start=True, stop=True).then_inc(s["count_done"], 1)

            te.wait_ge(s["table_done"], 1)
            load = lambda row, i, top: te.value_load(table[0:1, row, bass.ds(i, 1)], min_val=0, max_val=top)

            def rows_t(i, n, par):
                te.wait_ge(row_s[par], 16 * n)
                if not (isinstance(i, int) and i == 0):
                    te.wait_ge(s["xT_used"], i)
                for c in range(C):
                    ins = te.transpose(bank(4)[:, c * P:(c + 1) * P], grow[par][:, c * P:(c + 1) * P], idn[:, :])
                    if isinstance(i, int) and i == 0 and c == 0:
                        ins.then_inc(s["slot_down"], 1)
                ins.then_inc(s["xT_done"], 1)

            def experts_up(i, par):
                loads, off = load(3, i, 32 * E), load(1, i, EXPERT)
                te.wait_ge(wl, loads)
                te.wait_ge(s["xT_used"], i + 1)
                te.wait_ge(s["act_done"], i + 1)
                for c in range(C):
                    for n in range(2 * I // NT):
                        ins = te.matmul(bank(n), xTt[par][:, c, :], weights[:, bass.ds(off + (2 * c * I + n * NT), NT)],
                                        start=(c == 0), stop=(c == C - 1))
                ins.then_inc(s["up_done"], 1)

            def experts_down(i, par):
                off = load(1, i, EXPERT)
                te.wait_ge(s["aT_used"], i + 1)
                te.wait_ge(s["y_ready"], i + 1)
                for c in range(IC):
                    ins = te.matmul(bank(7), aTt[par][:, c, :], weights[:, bass.ds(off + (2 * C * I + c * D), D)],
                                    start=(c == 0), stop=(c == IC - 1))
                ins.then_inc(s["slot_down"], 1)

            def hidden_t(i):
                te.wait_ge(s["act_done"], i + 2)
                if not (isinstance(i, int) and i == 0):
                    te.wait_ge(s["aT_used"], i)
                for c in range(IC):
                    ins = te.transpose(bank(5 + c // C)[:, c % C * P:(c % C + 1) * P], sil[1][:, c * P:(c + 1) * P], idn[:, :])
                ins.then_inc(s["aT_done"], 1)

            def block(i, n, par):
                experts_up(i, par)
                rows_t(i + 1, n, 1 - par)
                if not (isinstance(i, int) and i == 0):
                    experts_down(i - 1, 1 - par)
                hidden_t(i)

            rows_t(0, 1, 0)
            block(0, 1, 0)
            with te.Fori(0, (SLOTS - 1) // 2, 1) as m:
                block(2 * m + 1, m + 2, 1)
                block(2 * m + 2, m + 2, 0)
            experts_down(SLOTS - 1, 0)


def kernel(**inputs):
    import numpy as np
    import concourse.bacc as bacc
    from concourse.bass_utils import run_bass_kernel_spmd as launch

    a = {k: np.asarray(v) for k, v in inputs.items()}

    def channel_major(v):
        return v.reshape(NG, NB, T, C, P).transpose(0, 4, 3, 1, 2).reshape(NG, P, W)

    def cols(v):
        return v.reshape(C, P).T

    def rows_first(w, chunks):
        return w.T.reshape(chunks, P, w.shape[0]).transpose(1, 0, 2)

    h = np.array([[1.0]], np.float32)
    while h.shape[0] < P:
        h = np.block([[h, h], [h, -h]])
    lower = np.arange(P)
    wide = lambda v, dt: np.broadcast_to(np.asarray(v, dt), (P, len(v)))
    w1 = a["L1_ffn_w1"].transpose(0, 2, 1).reshape(E, C, P, I)
    w3 = a["L1_ffn_w3"].transpose(0, 2, 1).reshape(E, C, P, I)
    arrays = {
        "x_cm": channel_major(a["x"]),
        "ctx_cm": channel_major(a["ctx_2048"]),
        "vecs": np.stack([cols(a[n]) for n in ("L0_xattn_w", "L0_xattn_u", "L1_xattn_time_decay", "L1_xattn_time_first")], 1),
        "gains": np.broadcast_to(np.concatenate([a["g_xattn"], a["g_ffn"]]), (P, 4)),
        "w1t": rows_first(a["L0_ffn_W1"], C),
        "w3t": rows_first(a["L0_ffn_W3"], C),
        "w2t": rows_first(a["L0_ffn_W2"], J),
        "gate_t": rows_first(a["L1_ffn_gate_w"], C),
        "e13": np.concatenate([w1, w3], 3).transpose(0, 2, 1, 3).reshape(E, P, 2 * C * I),
        "e2": a["L1_ffn_w2"].transpose(0, 2, 1).reshape(E, IC, P, D).transpose(0, 2, 1, 3).reshape(E, P, IC * D),
        "had": np.stack([h, -h], 1).astype(np.float16),
        "ones_mean": np.full((P, P), 1.0 / D, np.float32),
        "ident": np.eye(P, dtype=np.float32),
        "tri": (lower[:, None] < lower[None, :]).astype(np.float16),
        "ones16": np.ones((P, P), np.float16),
        "tok_id": np.stack([np.broadcast_to(lower[:, None] + P * np.arange(TOK // P), (2, P, TOK // P)).transpose(1, 0, 2),
                            np.zeros((P, 2, TOK // P), np.int64)], 3).astype(np.int32),
        "ebase": wide(TOK * np.arange(E), np.float32),
        "desc": wide(E - np.arange(E), np.float32),
        "blocks": wide(P * np.arange(16), np.float32),
        "slot_no": wide(np.arange(SLOTS + 1), np.float32),
        "spare_rows": np.stack([TOK + np.arange(LIST) % P, np.zeros(LIST, np.int64)], 1).astype(np.int32).reshape(P, 2 * LIST // P),
        "zero_rows": np.zeros((P, D), np.float32),
    }
    arrays = {k: np.ascontiguousarray(v) for k, v in arrays.items()}
    nc = bacc.Bacc("TRN2", target_bir_lowering=False, num_devices=1)
    args = [nc.dram_tensor(n, v.shape, mybir.dt.from_np(v.dtype), kind="ExternalInput").ap() for n, v in arrays.items()]
    out = nc.dram_tensor("out", (TOK + P, D), F32, kind="ExternalOutput").ap()
    build(nc, *args, out)
    r = launch(nc, [arrays], core_ids=[0])
    return r.results[0]["out"][:TOK].reshape(BATCH, T, D)
```

```python
from contextlib import ExitStack

import concourse.bass as bass
from concourse import mybir

F32 = mybir.dt.float32
F16 = mybir.dt.float16
I32 = mybir.dt.int32
ALU = mybir.AluOpType
ACT = mybir.ActivationFunctionType
AX = mybir.AxisListType.X

P = 128
BATCH, T, D = 8, 256, 512
TOK = BATCH * T
NT = 512
NG = TOK // NT
NB = NT // T
C = D // P
W = C * NT
H = 2048
J = H // P
E, I = 8, 1024
IC = I // P
TILES = NT // P
EPS = 1e-5
JITTER2 = 0.02

SW = 256.0
SX = 64.0
SH = 16.0

SLOTS = 2 * TOK // P + E - 1
SPARE = (SLOTS - 2 * TOK // P) * P
LIST = E * TOK + SPARE + P
EXPERT = 2 * C * I + IC * D
U = NT
EU = EXPERT // U
NU = E * EU
CHUNK_UNITS = [4, 3, 2, 3, 3, 2, 4, 3, 4, 3, 2, 3, 3, 2, 4, 3]
assert NG * sum(CHUNK_UNITS) == NU
ADD, SUB, MUL, MAXO = ALU.add, ALU.subtract, ALU.mult, ALU.max

BRANCHES = [("pre", 0)]
for _g in range(NG):
    if _g + 1 < NG:
        BRANCHES.append(("pre", _g + 1))
    if _g >= 1:
        BRANCHES.append(("post", _g - 1))
BRANCHES.append(("post", NG - 1))
NORMS = [(k, g, i) for k, g in BRANCHES for i in range(2 if k == "pre" else 1)]

BESIDE = [[("pre", 1, "sums")], [("pre", 1, "norm")], [("pre", 1, "exps"), ("post", -2, "rank")], [("pre", 1, "scan")],
          [("pre", 1, "den")], [("pre", 1, "mix")], [("pre", 1, "sums2")], [("pre", 1, "norm2")],
          [("pre", 1, "low"), ("post", -1, "sums")], [("post", -1, "norm")], [("post", -1, "exps")],
          [("post", -1, "scan")], [("post", -1, "den")], [("post", -1, "mix")], [("post", -1, "rows")],
          [("post", -1, "gate")]]
PROLOGUE = ["sums", ("q", 0), "norm", ("q", 1), ("w", 0), "router", ("q", 2), "exps", "scan", ("w", 1), ("w", 2), ("q", 3),
            "den", ("w", 3), "mix", ("w", 4), ("w", 5), ("h", 0), "next groups", "sums2", ("h", 1), ("w", 6), "norm2",
            ("h", 2), ("w", 7), "low", ("h", 3)]
EPILOGUE = [("post", NG - 1, s) for s in ("sums", "norm", "exps")] + [("post", NG - 2, "rank")] + \
           [("post", NG - 1, s) for s in ("scan", "den", "mix", "rows", "gate", "rank")]


def branch_index(kind, g):
    return BRANCHES.index((kind, g))


def norm_index(kind, g, i):
    return NORMS.index((kind, g, i))


def steps_beside(g, j):
    return [(kind, g + d, step) for kind, d, step in BESIDE[j] if 0 <= g + d < NG]


def slot_units(g, j):
    n = g * sum(CHUNK_UNITS) + sum(CHUNK_UNITS[:j])
    return range(n, n + CHUNK_UNITS[j])


def build(nc, x_cm, ctx_cm, vecs, gains, w1t, w3t, w2t, gate_t, ew, had, ones_mean, ident,
          tri, ones16, tok_id, ebase, desc, blocks, slot_no, spare_rows, zero_rows, out):
    ctx = ExitStack()
    with ctx:
        def sb(name, shape, dt):
            return ctx.enter_context(nc.sbuf_tensor(name, shape, dt))

        def sem(name):
            return ctx.enter_context(nc.semaphore(name))

        xn_rows = nc.dram_tensor("xn_rows", (TOK + P, D), F32).ap()
        e16 = nc.dram_tensor("e16", (NU * P, 2 * U), F16).ap()
        row_list = nc.dram_tensor("row_list", (LIST, 2), I32).ap()

        weights = sb("weights", [P, 2 * EXPERT], F32)
        w16 = weights[:, :].bitcast(F16)
        n1 = 2 * C * H
        w1s = w16[:, 0:n1].rearrange("p (s c h) -> p s c h", s=2, c=C)
        w3s = w16[:, n1:2 * n1].rearrange("p (s c h) -> p s c h", s=2, c=C)
        w2s = w16[:, 2 * n1:2 * n1 + 2 * J * D].rearrange("p (s j d) -> p s j d", s=2, j=J)
        X = sb("X", [P, 3, C, NT], F32)
        V = sb("V", [P, W], F32)
        K = sb("K", [P, W], F32)
        E1 = sb("E1", [P, W], F32)
        E2 = sb("E2", [P, W], F32)
        SPs = sb("SPs", [P, W], F32)
        SQs = sb("SQs", [P, W], F32)
        xs = sb("xs", [P, 2, 2, C, NT], F16)
        work = sb("work", [P, 4 * NT], F32)
        sg = work[:, 0:2 * NT].rearrange("p (a n) -> p a n", a=2)
        raw = work[:, 2 * NT:4 * NT].rearrange("p (a n) -> p a n", a=2)
        halves = sb("halves", [P, 2, 2, U], F16)
        hs = sb("hs", [P, 2, 2, NT], F16)
        vec = sb("vec", [P, 4, C], F32)
        dec = sb("dec", [P, 2, C], F32)
        nm = sb("nm", [P, 2, C], F32)
        um = sb("um", [P, 2, C], F32)
        gn = sb("gn", [P, 4], F32)
        sc = sb("sc", [P, 4], F32)
        eps = sb("eps", [P, 1], F32)
        one = sb("one", [P, 1], F32)
        hads = sb("hads", [P, 2, P], F16)
        onesm = sb("onesm", [P, P], F32)
        idn = sb("idn", [P, P], F32)
        tris = sb("tris", [P, P], F16)
        ones1 = sb("ones1", [P, P], F16)
        gw = sb("gw", [P, C, E], F32)
        gsum = sb("gsum", [P, E], F32)
        entry = sb("entry", [P, 2, TOK // P, 2], I32)
        ebs = sb("ebs", [P, E], F32)
        dsc = sb("dsc", [P, E], F32)
        blk = sb("blk", [P, 16], F32)
        sno = sb("sno", [P, SLOTS + 1], F32)
        st = sb("st", [P, TILES, 6], F32)
        mv = sb("mv", [P, TILES, 2], F32)
        rt = sb("rt", [P, 4, TILES], F32)
        q = [sb(f"q{n}", [P, TILES, E], F32) for n in range(10)]
        r4 = [sb(f"r4_{n}", [P, TILES], F32) for n in range(6)]
        a16 = sb("a16", [P, 2, TILES, E], F16)
        cum = sb("cum", [P, E], F32)
        pos = sb("pos", [P, 2, TOK // P], I32)
        cnt = sb("cnt", [P, 6, E], F32)
        cmp16 = sb("cmp16", [P, E, 16], F32)
        sl = sb("sl", [P, 4, SLOTS + 1], F32)
        sle = work[:, 0:(SLOTS + 1) * E].rearrange("p (s e) -> p s e", e=E)
        table = sb("table", [P, 4, SLOTS + 1], I32)
        idxt = sb("idxt", [P, 2, 2], I32)
        outl = sb("outl", [P, 2, 2], I32)
        starts = sb("starts", [P, E], I32)

        PS = ctx.enter_context(nc.psum_tensor("PS", [P, 8, NT], F32))
        bank = lambda n: PS[:, n, :]
        ABANK, BBANK, OUT0, S0, S1 = 0, 1, 2, 6, 7

        names = """const_in hot_in gains_th scal_ready decay_a dec_ready gsum_ready gmean_ready gw_ready zeroed
            w_hi w_lo q_bf q_hi q_lo xsum_done kc_done p_done num_done y_done had_out had_hi had_lo spare_in
            v_in v_used sq_done sums_done stat_done msq_done var_done r0_done k_done xh_done xs_ready
            e1_done e2_done ev1_done ev2_done q_done den_done rec_done wkv_done
            a_done b_done sig_done s_done hid_done hh_done hl_done down_done out_done resid_done
            lg_done tr_done xt_done raw_done tvar_done tr0_done xn_done x3_out xn_out d_done ex_done
            asg_done rank_done pos_done scat_done cum_done count_done table_done
            idx_in rows_in xT_done xT_used xTl_done up_done act_done slot_down aT_done aT_used aTl_done unit_hi unit_lo
            y_ready gathers g1_done sil_done sig_steps vchain achain gchain""".split()
        s = {n: sem(n) for n in names}
        x_in = [sem(f"x_in{n}") for n in range(3)]
        w_in = [sem(f"w_in{n}") for n in range(2)]
        q_in = [sem(f"q_in{n}") for n in range(2)]
        wl = [sem(f"expert_in{n}") for n in range(2)]
        unit_in = [sem(f"unit_in{n}") for n in range(2)]
        unit_out = [sem(f"unit_out{n}") for n in range(2)]
        idx_s = [sem(f"idx_in{n}") for n in range(2)]
        row_s = [sem(f"rows_in{n}") for n in range(2)]
        ysto = [sem(f"y_store{n}") for n in range(2)]
        out_s = [sem(f"out_in{n}") for n in range(2)]

        entry_w = entry[:, :, :, :].bitcast(F32)
        outl_w = outl[:, :, :].bitcast(F32)
        xg = lambda g: X[:, g % 3, :, :].rearrange("p c n -> p (c n)")
        ch = lambda t, c: t[:, c * NT:(c + 1) * NT]
        seq = lambda t: t[:, :].rearrange("p (a t) -> p a t", t=T)
        later = lambda t: seq(t)[:, :, 1:T]
        before = lambda t: seq(t)[:, :, 0:T - 1]
        wide = lambda t: t.rearrange("p (o n) -> p o n", o=1).to_broadcast([P, C, NT])
        cn = lambda t: t.rearrange("p (c n) -> p c n", c=C)
        M_, MSQ, VAR, RS = (E1[:, n * NT:(n + 1) * NT] for n in range(4))
        wstage = [work[:, :], xs[:, 0, :, :, :].rearrange("p a c n -> p (a c n)").bitcast(F32)]
        qstage = [X[:, 1 + n, :, :].rearrange("p c n -> p (c n)") for n in range(2)]
        qtmp = xs[:, 1, :, :, :].rearrange("p a c n -> p (a c n)").bitcast(F32)
        NW, NQ = 2 * C, 4

        def w_dst(u, half):
            return (w1s, w3s)[u // C][:, half, u % C, :]

        def q_dst(u, half):
            return w2s[:, half, 4 * u:4 * u + 4, :].rearrange("p j d -> p (j d)")

        blockv = ctx.enter_context(nc.Block())
        CONSTS = [(hads[:, :, :], had), (idn[:, :], ident), (tris[:, :], tri), (ones1[:, :], ones16),
                  (entry[:, :, :, :], tok_id), (ebs[:, :], ebase), (dsc[:, :], desc), (blk[:, :], blocks),
                  (sno[:, :], slot_no), (gw[:, :, :], gate_t)]
        posts_before = lambda b: sum(kind == "post" for kind, _ in BRANCHES[:b])

        grow = [SPs[:, n * D:(n + 1) * D] for n in range(2)]
        xTt = [SPs[:, (2 + n) * D:(3 + n) * D].bitcast(F16).rearrange("p (s c n) -> p s c n", s=2, c=C) for n in range(2)]
        sil = [K[:, 0:I], K[:, I:2 * I]]
        aTt = [SQs[:, n * I:(n + 1) * I].bitcast(F16).rearrange("p (s c n) -> p s c n", s=2, c=IC) for n in range(2)]
        xTp = PS[:, 4, :].rearrange("p (c n) -> p c n", c=C)
        aTp = PS[:, 5:7, :].rearrange("p b n -> p (b n)").rearrange("p (c n) -> p c n", c=IC)
        yt = [V[:, n * D:(n + 1) * D] for n in range(2)]

        @blockv.sync
        def _(sp):
            sp.dma_start(vec[:, :, :], vecs).then_inc(s["hot_in"], 16)
            sp.dma_start(gn[:, :], gains).then_inc(s["hot_in"], 16)
            sp.dma_start(onesm[:, :], ones_mean).then_inc(s["hot_in"], 16)
            sp.dma_start(xg(0), x_cm[0, :, :]).then_inc(x_in[0], 16)
            sp.dma_start(V[:, :], ctx_cm[0, :, :]).then_inc(s["v_in"], 16)

            def load_w(u):
                if u >= 2:
                    sp.wait_ge(s["w_lo"], u - 1)
                sp.dma_start(wstage[u % 2], (w1t, w3t)[u // C][:, u % C, :]).then_inc(w_in[u % 2], 16)

            def load_q(u):
                if u >= 2:
                    sp.wait_ge(s["q_lo"], u - 1)
                sp.dma_start(qstage[u % 2], w2t[:, 4 * u:4 * u + 4, :].rearrange("p j d -> p (j d)")).then_inc(q_in[u % 2], 16)

            load_q(0)
            load_q(1)
            load_w(0)
            load_w(1)
            for t, a in CONSTS:
                sp.dma_start(t, a).then_inc(s["const_in"], 16)
            for item in [x for x in PROLOGUE if isinstance(x, tuple)]:
                if item[0] == "w" and item[1] + 2 < NW:
                    load_w(item[1] + 2)
                if item[0] == "q" and item[1] + 2 < NQ:
                    load_q(item[1] + 2)
            sp.dma_start(row_list.rearrange("(p n) o -> p (n o)", p=P), spare_rows).then_inc(s["spare_in"], 16)
            sp.dma_start(xn_rows[TOK:TOK + P, :], zero_rows).then_inc(s["spare_in"], 16)
            sp.dma_start(out[TOK:TOK + P, :], zero_rows).then_inc(s["spare_in"], 16)
            def load_unit(u, par):
                sp.dma_start(raw[:, par, :], ew[bass.ds(u * P, P), :]).then_inc(unit_in[par], 16)

            def store_unit(u, par):
                sp.wait_ge(s["unit_lo"], u + 1)
                sp.dma_start(e16[bass.ds(u * P, P), :], halves[:, par, :, :].rearrange("p s n -> p (s n)")).then_inc(unit_out[par], 16)

            sp.wait_ge(s["w_lo"], NW)
            load_unit(0, 0)
            load_unit(1, 1)
            with sp.Fori(0, NU // 2 - 1, 1) as m:
                for par in range(2):
                    store_unit(2 * m + par, par)
                    load_unit(2 * m + 2 + par, par)
            for par in range(2):
                store_unit(NU - 2 + par, par)
            for par in range(2):
                sp.wait_ge(unit_out[par], 16 * (NU // 2))
            sp.wait_ge(s["down_done"], NG * J)
            pieces = EU // 2
            wreg = w16.rearrange("p (b c n) -> p b c n", b=2, c=pieces)
            e16v = e16.rearrange("(e c u p) n -> e c p u n", e=E, c=pieces, u=2)

            def load_piece(e, c, par):
                sp.dma_start(wreg[:, e % 2, bass.ds(c, 1), :].rearrange("p o (u n) -> p (o u) n", u=2),
                             e16v[e, bass.ds(c, 1), :, :, :].rearrange("o p u n -> p (o u) n")).then_inc(wl[par], 16)

            for e in range(E):
                if e == 2:
                    sp.wait_ge(s["table_done"], 1)
                if e >= 2:
                    first = sp.value_load(starts[0:1, e - 2:e - 1], min_val=1, max_val=SLOTS + 1)
                    sp.wait_ge(s["slot_down"], first)
                before = 16 * (pieces // 2) * e
                for par in range(2):
                    if e >= 1:
                        sp.wait_ge(wl[par], before)
                    load_piece(e, par, par)
                with sp.Fori(1, pieces // 2, 1) as m:
                    for par in range(2):
                        sp.wait_ge(wl[par], before + 16 * m)
                        load_piece(e, 2 * m + par, par)

        @blockv.gpsimd
        def _(gp):
            chain = [0]

            def link(ins):
                chain[0] += 1
                ins.then_inc(s["gchain"], 1)
                gp.wait_ge(s["gchain"], chain[0])

            def butterflies(u):
                a = qstage[u % 2]
                gp.wait_ge(q_in[u % 2], 16 * (u // 2 + 1))
                b4 = qtmp.rearrange("p (b a d) -> p b a d", b=2, a=2)
                a4 = a.rearrange("p (b a d) -> p b a d", b=2, a=2)
                link(gp.tensor_tensor(b4[:, :, 0, :], a4[:, :, 0, :], a4[:, :, 1, :], ADD))
                link(gp.tensor_tensor(b4[:, :, 1, :], a4[:, :, 0, :], a4[:, :, 1, :], SUB))
                link(gp.tensor_tensor(a[:, 0:2 * D], qtmp[:, 0:2 * D], qtmp[:, 2 * D:4 * D], ADD))
                gp.tensor_tensor(a[:, 2 * D:4 * D], qtmp[:, 0:2 * D], qtmp[:, 2 * D:4 * D], SUB).then_inc(s["q_bf"], 1)
                gp.wait_ge(s["q_bf"], u + 1)

            def xsum(kind, g, second):
                b, n = branch_index(kind, g), norm_index(kind, g, int(second))
                if b + second:
                    gp.wait_ge(s["wkv_done"], b + second)
                if n >= 1:
                    gp.wait_ge(s["stat_done"], n)
                    gp.wait_ge(s["xsum_done"], n)
                if kind == "pre" and not second:
                    gp.wait_ge(x_in[g % 3], 16 * (g // 3 + 1))
                if kind == "post":
                    gp.wait_ge(s["resid_done"], g + 1)
                xv = xg(g)
                link(gp.tensor_tensor(E2[:, 0:2 * NT], xv[:, 0:2 * NT], xv[:, 2 * NT:4 * NT], ADD))
                gp.tensor_tensor(E2[:, 2 * NT:3 * NT], E2[:, 0:NT], E2[:, NT:2 * NT], ADD).then_inc(s["xsum_done"], 1)

            def centre(kind, g, second):
                b, n = branch_index(kind, g), norm_index(kind, g, int(second))
                gp.wait_ge(s["msq_done"], n + 1)
                if posts_before(b):
                    gp.wait_ge(s["xn_out"], 16 * posts_before(b))
                gp.tensor_tensor(cn(K[:, :]), cn(xg(g)), wide(M_), SUB).then_inc(s["kc_done"], 1)

            def numerator(b):
                gp.wait_ge(s["p_done"], b + 1)
                gp.wait_ge(s["ev2_done"], b + 1)
                gp.tensor_tensor(later(E1), later(E1), before(SPs), ADD).then_inc(s["num_done"], 1)

            def update(kind, g):
                b = branch_index(kind, g)
                gp.wait_ge(s["v_used"], b + 1)
                gp.wait_ge(s["y_done"], b + 1)
                gp.tensor_tensor(xg(g), xg(g), E1[:, :], ADD).then_inc(s["wkv_done"], 1)
                gp.wait_ge(s["wkv_done"], b + 1)

            def low(g):
                gp.wait_ge(s["xh_done"], g + 1)
                gp.wait_ge(s["k_done"], norm_index("pre", g, 1) + 1)
                f = lambda half: xs[:, g % 2, half, :, :].rearrange("p c n -> p (c n)")
                gp.tensor_tensor(f(1), K[:, :], f(0), SUB).then_inc(s["xs_ready"], 1)

            def products(b):
                gp.wait_ge(s["v_in"], 16 * (b + 1))
                gp.wait_ge(s["e1_done"], b + 1)
                gp.wait_ge(s["e2_done"], b + 1)
                gp.tensor_tensor(K[:, :], E1[:, :], V[:, :], MUL).then_inc(s["ev1_done"], 1)
                gp.wait_ge(s["q_done"], b + 1)
                gp.wait_ge(s["ev1_done"], b + 1)
                gp.tensor_tensor(E1[:, :], E2[:, :], V[:, :], MUL).then_inc(s["ev2_done"], 1)

            def scatter(g):
                gp.wait_ge(s["spare_in"], 48)
                gp.wait_ge(s["pos_done"], g + 1)
                gp.wait_ge(s["const_in"], 16 * len(CONSTS))
                for i in range(g * TILES, (g + 1) * TILES):
                    for k in range(2):
                        gp.indirect_dma_start(row_list, bass.IndirectOffsetOnAxis(ap=pos[:, k, i:i + 1], axis=0),
                                              entry[:, k, i, :], None).then_inc(s["scat_done"], 16)

            def run(kind, g, step):
                if step in ("sums", "sums2"):
                    xsum(kind, g, step == "sums2")
                if step in ("norm", "norm2"):
                    centre(kind, g, step == "norm2")
                if step == "low":
                    low(g)
                if step == "mix":
                    update(kind, g)
                if step == "exps":
                    products(branch_index(kind, g))
                if step == "scan":
                    numerator(branch_index(kind, g))
                if step == "rank":
                    scatter(g)

            for item in PROLOGUE:
                if isinstance(item, str):
                    run("pre", 0, item)
                elif item[0] == "q":
                    butterflies(item[1])
            for g in range(NG):
                for j in range(J):
                    for step in steps_beside(g, j):
                        run(*step)
            for step in EPILOGUE:
                run(*step)

            gp.wait_ge(s["table_done"], 1)
            gp.wait_ge(s["scat_done"], 16 * 2 * TOK // P)
            gp.wait_ge(s["xn_out"], 16 * NG)
            gp.wait_ge(s["wkv_done"], len(BRANCHES))

            def first_row(i):
                return gp.value_load(table[0:1, 2, bass.ds(i, 1)], min_val=0, max_val=LIST - P)

            def load_list(i, n, par):
                gp.dma_start(idxt[:, par, :], row_list[bass.ds(first_row(i), P), :]).then_inc(idx_s[par], 16)

            def load_out_list(i, par):
                gp.dma_start(outl[:, par, :], row_list[bass.ds(first_row(i), P), :]).then_inc(out_s[par], 16)

            def gather(i, n, par):
                gp.wait_ge(idx_s[par], 16 * n)
                gp.sem_inc(s["gathers"], 1)
                gp.indirect_dma_start(grow[par], None, xn_rows, bass.IndirectOffsetOnAxis(ap=idxt[:, par, 0:1], axis=0)).then_inc(row_s[par], 16)

            def add_out(i, n, par, last=False):
                if not (isinstance(i, int) and i == 0):
                    gp.wait_ge(ysto[1 - par], 16 * (n - 1 + par))
                    gp.sem_inc(s["gathers"], 1)
                if not last:
                    load_out_list(i + 1, 1 - par)
                gp.wait_ge(s["y_ready"], i + 2)
                gp.sem_inc(s["gathers"], 1)
                gp.indirect_dma_start(out, bass.IndirectOffsetOnAxis(ap=outl[:, par, 0:1], axis=0), yt[par], None, compute_op=ADD).then_inc(ysto[par], 16)

            gp.wait_ge(s["x3_out"], 16 * NG)
            load_list(0, 1, 0)
            load_list(1, 1, 1)
            load_out_list(0, 0)
            gather(0, 1, 0)
            gather(1, 1, 1)

            def block(i, n, par):
                gp.wait_ge(row_s[par], 16 * n)
                gp.sem_inc(s["gathers"], 1)
                load_list(i + 2, n + 1, par)
                gp.wait_ge(s["xT_done"], i + 1)
                gather(i + 2, n + 1, par)
                add_out(i, n, par)

            block(0, 1, 0)
            block(1, 1, 1)
            with gp.Fori(1, (SLOTS - 1) // 2, 1) as m:
                block(2 * m, m + 1, 0)
                block(2 * m + 1, m + 1, 1)
            n = (SLOTS - 1) // 2
            add_out(2 * n, n + 1, 0, last=True)
            gp.wait_ge(row_s[0], 16 * (n + 1))
            gp.wait_ge(row_s[1], 16 * (n + 1))
            for k in range(2):
                gp.wait_ge(ysto[k], 16 * (n + 1 - k))

        @blockv.scalar
        def _(act):
            chain = [0]

            def link(ins):
                chain[0] += 1
                ins.then_inc(s["achain"], 1)
                act.wait_ge(s["achain"], chain[0])

            act.wait_ge(s["hot_in"], 48)
            act.activation(gn[:, :], gn[:, :], ACT.Tanh).then_inc(s["gains_th"], 1)
            act.preload_act_table_set("natural_log_exp_and_others")
            act.wait_ge(s["zeroed"], 2)
            link(act.activation(vec[:, 2, :], vec[:, 2, :], ACT.Exp))
            act.activation(dec[:, 0, :], vec[:, 0, :], ACT.Exp)
            act.activation(dec[:, 1, :], vec[:, 2, :], ACT.Exp, scale=-1.0).then_inc(s["dec_ready"], 1)

            def load_v(b):
                if b < len(BRANCHES):
                    act.wait_ge(s["v_used"], b)
                    act.dma_start(V[:, :], ctx_cm[BRANCHES[b][1], :, :]).then_inc(s["v_in"], 16)

            def unit_high(u):
                act.wait_ge(unit_in[u % 2], 16 * (u // 2 + 1))
                if u >= 2:
                    act.wait_ge(unit_out[u % 2], 16 * (u // 2))
                act.activation(halves[:, u % 2, 0, :], raw[:, u % 2, :], ACT.Copy, scale=SW).then_inc(s["unit_hi"], 1)

            def w_high(u):
                act.wait_ge(w_in[u % 2], 16 * (u // 2 + 1))
                act.activation(w_dst(u, 0), wstage[u % 2], ACT.Copy, scale=SW).then_inc(s["w_hi"], 1)

            def q_high(u):
                act.wait_ge(s["q_bf"], u + 1)
                act.activation(q_dst(u, 0), qstage[u % 2], ACT.Copy, scale=SW).then_inc(s["q_hi"], 1)

            def had_high(jj):
                act.wait_ge(s["had_out"], jj + 1)
                for a in range(4):
                    ins = act.activation(w2s[:, 0, 4 * a + jj, :], bank(OUT0 + a), ACT.Copy, scale=float(H) ** -0.5)
                ins.then_inc(s["had_hi"], 1)

            def run(kind, g, step):
                b = branch_index(kind, g)
                layer = 0 if kind == "pre" else 1
                second = step.endswith("2")
                if step in ("sums", "sums2", "norm", "norm2"):
                    n = norm_index(kind, g, int(second))
                if step in ("sums", "sums2"):
                    if second:
                        act.wait_ge(s["wkv_done"], b + 1)
                    else:
                        if b >= 1:
                            act.wait_ge(s["wkv_done"], b)
                        if kind == "pre":
                            act.wait_ge(x_in[g % 3], 16 * (g // 3 + 1))
                        else:
                            act.wait_ge(s["resid_done"], g + 1)
                    act.activation(SPs[:, :], xg(g), ACT.Square).then_inc(s["sq_done"], 1)
                    if second:
                        load_v(b + 1)
                elif step in ("norm", "norm2"):
                    if posts_before(b):
                        act.wait_ge(s["x3_out"], 16 * posts_before(b))
                    act.wait_ge(s["stat_done"], n + 1)
                    act.activation(M_, bank(S0), ACT.Copy)
                    act.activation(MSQ, bank(S0), ACT.Square).then_inc(s["msq_done"], 1)
                    act.wait_ge(s["var_done"], n + 1)
                    link(act.activation(RS, VAR, ACT.Ln, bias=eps[:, 0:1]))
                    act.activation(RS, RS, ACT.Exp, scale=-0.5).then_inc(s["r0_done"], 1)
                elif step == "low":
                    act.wait_ge(s["k_done"], norm_index(kind, g, 1) + 1)
                    if g == 0:
                        act.wait_ge(s["w_lo"], NW)
                    if g >= 2:
                        act.wait_ge(s["b_done"], J * (g - 1))
                    act.activation(xs[:, g % 2, 0, :, :].rearrange("p c n -> p (c n)"), K[:, :], ACT.Copy).then_inc(s["xh_done"], 1)
                elif step == "exps":
                    n = norm_index(kind, g, 0)
                    act.wait_ge(s["k_done"], n + 1)
                    for c in range(C):
                        ins = act.activation(ch(E1, c), ch(K, c), ACT.Exp, bias=nm[:, layer, c:c + 1])
                    ins.then_inc(s["e1_done"], 1)
                    for c in range(C):
                        ins = act.activation(ch(E2, c), ch(K, c), ACT.Exp, bias=um[:, layer, c:c + 1])
                    ins.then_inc(s["e2_done"], 1)
                elif step == "den":
                    act.wait_ge(s["den_done"], b + 1)
                    act.wait_ge(s["ev2_done"], b + 1)
                    link(act.activation(later(E2), later(K), ACT.Ln))
                    act.activation(later(E2), later(E2), ACT.Exp, scale=-1.0).then_inc(s["rec_done"], 1)
                elif step == "rows":
                    load_v(b + 1)
                    for i in range(TILES):
                        act.wait_ge(s["tr_done"], TILES * g + i + 1)
                        act.activation(E1[:, i * D:(i + 1) * D], bank(S0 + i % 2), ACT.Copy).then_inc(s["xt_done"], 1)
                    if g + 3 < NG:
                        act.dma_start(xg(g + 3), x_cm[g + 3, :, :]).then_inc(x_in[g % 3], 16)
                    act.wait_ge(s["xt_done"], TILES * (g + 1))
                    act.dma_start(out[g * NT:(g + 1) * NT, :].rearrange("(i p) d -> p i d", p=P), cn(E1[:, :])).then_inc(s["x3_out"], 16)
                elif step == "gate":
                    act.wait_ge(s["tvar_done"], g + 1)
                    link(act.activation(rt[:, 0, :], mv[:, :, 1], ACT.Ln, bias=eps[:, 0:1]))
                    act.activation(rt[:, 0, :], rt[:, 0, :], ACT.Exp, scale=-0.5).then_inc(s["tr0_done"], 1)
                    act.wait_ge(s["d_done"], g + 1)
                    act.activation(q[4][:, :, :], q[4][:, :, :], ACT.Exp, scale=-1.0)
                    act.activation(q[5][:, :, :], q[5][:, :, :], ACT.Exp, scale=-1.0).then_inc(s["ex_done"], 1)
                    act.wait_ge(s["xn_done"], g + 1)
                    act.dma_start(xn_rows[g * NT:(g + 1) * NT, :].rearrange("(i p) d -> p i d", p=P), cn(K[:, :])).then_inc(s["xn_out"], 16)

            def chunk(g, j):
                n = J * g + j
                units = slot_units(g, j)
                unit_high(units[0])
                if n >= 2:
                    act.wait_ge(s["hl_done"], n - 1)
                act.wait_ge(s["a_done"], n + 1)
                link(act.activation(sg[:, j % 2, :], bank(ABANK), ACT.Exp, scale=-1.0 / (SW * SX)))
                link(act.activation(sg[:, j % 2, :], sg[:, j % 2, :], ACT.Ln, bias=one[:, 0:1]))
                act.activation(sg[:, j % 2, :], sg[:, j % 2, :], ACT.Exp, scale=-1.0).then_inc(s["sig_done"], 1)
                unit_high(units[1])
                if n >= 2:
                    act.wait_ge(s["down_done"], n - 1)
                act.wait_ge(s["hid_done"], n + 1)
                act.activation(hs[:, j % 2, 0, :], sg[:, j % 2, :], ACT.Copy).then_inc(s["hh_done"], 1)
                for u in units[2:]:
                    unit_high(u)

            for item in PROLOGUE:
                if item == "next groups":
                    act.wait_ge(s["q_lo"], NQ)
                    for g in (1, 2):
                        act.dma_start(xg(g), x_cm[g, :, :]).then_inc(x_in[g], 16)
                elif isinstance(item, str):
                    run("pre", 0, item)
                else:
                    {"w": w_high, "q": q_high, "h": had_high}[item[0]](item[1])
            for g in range(NG):
                for j in range(J):
                    chunk(g, j)
                    for step in steps_beside(g, j):
                        run(*step)
            for step in EPILOGUE:
                run(*step)

            h1 = PS[:, 0:2, :].rearrange("p b n -> p (b n)")

            def block(i, par):
                act.wait_ge(s["up_done"], i + 1)
                act.wait_ge(s["act_done"], i + 1)
                act.activation(sil[0], h1, ACT.Exp, scale=-1.0 / (SW * SX)).then_inc(s["sig_steps"], 1)
                act.wait_ge(s["sig_steps"], 2 * i + 1)
                act.activation(sil[0], sil[0], ACT.Ln, bias=one[:, 0:1]).then_inc(s["sig_steps"], 1)
                act.wait_ge(s["sig_steps"], 2 * i + 2)
                act.activation(sil[0], sil[0], ACT.Exp, scale=-1.0).then_inc(s["sil_done"], 1)
                act.wait_ge(s["xT_done"], i + 2)
                act.activation(xTt[1 - par][:, 0, :, :], xTp, ACT.Copy, scale=SX).then_inc(s["xT_used"], 1)
                act.wait_ge(s["aT_done"], i + 1)
                if not (isinstance(i, int) and i == 0):
                    act.wait_ge(s["slot_down"], i)
                act.activation(aTt[par][:, 0, :, :], aTp, ACT.Copy).then_inc(s["aT_used"], 1)

            act.wait_ge(s["xn_out"], 16 * NG)
            act.wait_ge(s["xT_done"], 1)
            act.activation(xTt[0][:, 0, :, :], xTp, ACT.Copy, scale=SX).then_inc(s["xT_used"], 1)
            block(0, 0)
            with act.Fori(0, (SLOTS - 1) // 2, 1) as m:
                block(2 * m + 1, 1)
                block(2 * m + 2, 0)

        @blockv.vector
        def _(ve):
            chain = [0]

            def link(ins):
                chain[0] += 1
                ins.then_inc(s["vchain"], 1)
                ve.wait_ge(s["vchain"], chain[0])

            ve.memset(eps[:, :], EPS).then_inc(s["zeroed"], 1)
            ve.memset(one[:, :], 1.0).then_inc(s["zeroed"], 1)
            link(ve.memset(cum[:, :], 0.0))
            ve.wait_ge(s["hot_in"], 48)
            for lay in range(2):
                link(ve.tensor_scalar(nm[:, lay, :], vec[:, 1 + 2 * lay, :], 0.0, -1.0, MAXO, MUL))
                link(ve.tensor_tensor(um[:, lay, :], vec[:, 1 + 2 * lay, :], nm[:, lay, :], ADD))
            ve.wait_ge(s["gains_th"], 1)
            link(ve.tensor_scalar(sc[:, 0:2], gn[:, 0:2], -1.0, None, MUL))
            link(ve.tensor_scalar(sc[:, 2:3], gn[:, 2:3], 1.0 / (SW * SH), None, MUL))
            link(ve.tensor_scalar(sc[:, 3:4], gn[:, 3:4], 1.0 / (SW * SH), None, MUL))
            ve.wait_ge(s["dec_ready"], 1)

            def newton(r, tmp, var, scale):
                link(ve.tensor_tensor(tmp, r, r, MUL))
                link(ve.scalar_tensor_tensor(tmp, var, EPS, tmp, ADD, MUL))
                link(ve.tensor_scalar(tmp, tmp, -0.5 * scale, 1.5 * scale, MUL, ADD))
                link(ve.tensor_tensor(tmp, tmp, r, MUL))

            def run(kind, g, step):
                b = branch_index(kind, g)
                layer = 0 if kind == "pre" else 1
                second = step.endswith("2")
                if step in ("sums", "sums2", "norm", "norm2"):
                    n = norm_index(kind, g, int(second))
                if step in ("sums", "sums2"):
                    ve.wait_ge(s["sq_done"], n + 1)
                    if n >= 1:
                        ve.wait_ge(s["stat_done"], n)
                    link(ve.tensor_tensor(SPs[:, 0:2 * NT], SPs[:, 0:2 * NT], SPs[:, 2 * NT:4 * NT], ADD))
                    ve.tensor_tensor(E2[:, 3 * NT:4 * NT], SPs[:, 0:NT], SPs[:, NT:2 * NT], ADD).then_inc(s["sums_done"], 1)
                elif step in ("norm", "norm2"):
                    ve.wait_ge(s["msq_done"], n + 1)
                    ve.tensor_tensor(VAR, bank(S1), MSQ, SUB).then_inc(s["var_done"], 1)
                    ve.wait_ge(s["r0_done"], n + 1)
                    ve.wait_ge(s["var_done"], n + 1)
                    newton(RS, MSQ, VAR, SX if second else 1.0)
                    ve.wait_ge(s["kc_done"], n + 1)
                    ve.tensor_tensor(cn(K[:, :]), cn(K[:, :]), wide(MSQ), MUL).then_inc(s["k_done"], 1)
                elif step == "scan":
                    def scan(dst, src, last):
                        for a in range(C * NB):
                            c = a // NB
                            t = slice(a * T, (a + 1) * T)
                            ins = ve.tensor_tensor_scan(dst[:, t], dec[:, layer, c:c + 1].to_broadcast([P, T]), src[:, t], 0.0, MUL, ADD)
                        last(ins)

                    ve.wait_ge(s["e1_done"], b + 1)
                    scan(SQs, E1, lambda ins: ins.then_inc(s["q_done"], 1))
                    ve.wait_ge(s["ev1_done"], b + 1)
                    scan(SPs, K, lambda ins: ins.then_inc(s["p_done"], 1))
                elif step == "den":
                    ve.wait_ge(s["e2_done"], b + 1)
                    ve.wait_ge(s["q_done"], b + 1)
                    ve.wait_ge(s["p_done"], b + 1)
                    ve.tensor_tensor(later(K), later(E2), before(SQs), ADD).then_inc(s["den_done"], 1)
                elif step == "mix":
                    ve.wait_ge(s["rec_done"], b + 1)
                    ve.wait_ge(s["den_done"], b + 1)
                    link(ve.tensor_tensor(later(K), later(K), later(E2), MUL))
                    link(ve.scalar_tensor_tensor(later(K), later(K), -2.0, later(E2), ADD, MUL))
                    ve.wait_ge(s["num_done"], b + 1)
                    ve.tensor_scalar(seq(E1)[:, :, 0:1], seq(V)[:, :, 0:1], sc[:, layer:layer + 1], -1.0, MUL, MUL).then_inc(s["v_used"], 1)
                    ve.scalar_tensor_tensor(later(E1), later(K), sc[:, layer:layer + 1], later(E1), MUL, MUL).then_inc(s["y_done"], 1)
                elif step == "rows":
                    ve.wait_ge(s["lg_done"], g + 1)
                    ve.tensor_copy(q[0][:, :, :], bank(S1)[:, 0:TILES * E].rearrange("p (i e) -> p i e", e=E)).then_inc(s["raw_done"], 1)
                    for i in range(TILES):
                        ve.wait_ge(s["xt_done"], TILES * g + i + 1)
                        link(ve.bn_stats(st[:, i, :], E1[:, i * D:(i + 1) * D]))
                        ins = ve.bn_aggr(mv[:, i, :], st[:, i, :])
                    ins.then_inc(s["tvar_done"], 1)
                    ve.wait_ge(s["tvar_done"], g + 1)
                elif step == "gate":
                    ve.wait_ge(s["tr0_done"], g + 1)
                    newton(rt[:, 0, :], rt[:, 1, :], mv[:, :, 1], 1.0)
                    for i in range(TILES):
                        ins = ve.tensor_scalar(K[:, i * D:(i + 1) * D], E1[:, i * D:(i + 1) * D], mv[:, i, 0:1], rt[:, 1, i:i + 1], SUB, MUL)
                    ins.then_inc(s["xn_done"], 1)
                    wide_e = lambda t: t.rearrange("p (i o) -> p i o", o=1).to_broadcast([P, TILES, E])
                    wide_i = lambda t: t.rearrange("p (o e) -> p o e", o=1).to_broadcast([P, TILES, E])
                    tt = lambda o, a, bb, op: link(ve.tensor_tensor(o, a, bb, op))
                    lg, oh1, oh2, ml, d1, d2, keep1, keep2, f, tmp = (t[:, :, :] for t in q)
                    mx1, mx2, w_, sm, _, _ = (t[:, :] for t in r4)
                    rs = rt[:, 1, :]
                    tt(lg, lg, wide_e(rs), MUL)

                    def top(src, mx, oh):
                        link(ve.tensor_reduce(mx, src, AX, MAXO))
                        tt(tmp, src, wide_e(mx), ALU.is_equal)
                        tt(tmp, tmp, wide_i(dsc[:, :]), MUL)
                        link(ve.tensor_reduce(w_, tmp, AX, MAXO))
                        tt(oh, wide_e(w_), wide_i(dsc[:, :]), ALU.is_equal)

                    ve.wait_ge(s["const_in"], 16 * len(CONSTS))
                    top(lg, mx1, oh1)
                    link(ve.scalar_tensor_tensor(ml, oh1, -3e38, lg, MUL, ADD))
                    top(ml, mx2, oh2)
                    tt(d1, wide_e(mx1), lg, SUB)
                    tt(d2, wide_e(mx2), ml, SUB)
                    link(ve.scalar_tensor_tensor(f, lg, -1.0, lg, MUL, MAXO))
                    tt(tmp, f, wide_e(mx1), MAXO)
                    link(ve.scalar_tensor_tensor(keep1, tmp, JITTER2, d1, MUL, ALU.is_ge))
                    tt(tmp, f, wide_e(mx2), MAXO)
                    link(ve.scalar_tensor_tensor(keep2, tmp, JITTER2, d2, MUL, ALU.is_ge))
                    ve.tensor_tensor(f, oh1, oh2, ADD).then_inc(s["d_done"], 1)
                    ve.wait_ge(s["d_done"], g + 1)
                    for i in range(TILES):
                        link(ve.tensor_copy(a16[:, 1, i, :], cum[:, :]))
                        tt(cum[:, :], cum[:, :], q[8][:, i, :], ADD)
                    ve.tensor_copy(a16[:, 0, :, :], f).then_inc(s["asg_done"], 1)
                    ve.wait_ge(s["ex_done"], g + 1)
                    for k, (d, keep) in enumerate(((d1, keep1), (d2, keep2))):
                        tt(d, d, keep, MUL)
                        link(ve.tensor_reduce(sm, d, AX, ADD))
                        link(ve.reciprocal(sm, sm))
                        link(ve.tensor_scalar(entry_w[:, k, g * TILES:(g + 1) * TILES, 1], sm, sc[:, 3:4], None, MUL))
                elif step == "rank":
                    ve.wait_ge(s["rank_done"], g + 1)
                    rk = bank(S0)[:, 0:TILES * E].rearrange("p (i e) -> p i e", e=E)
                    wide_i = lambda t: t.rearrange("p (o e) -> p o e", o=1).to_broadcast([P, TILES, E])
                    _, oh1, oh2, _, _, _, _, _, f, tmp = (t[:, :, :] for t in q)
                    link(ve.tensor_tensor(f, rk, wide_i(ebs[:, :]), ADD))
                    for k, oh in enumerate((oh1, oh2)):
                        link(ve.tensor_tensor(tmp, oh, f, MUL))
                        link(ve.tensor_reduce(r4[3][:, :], tmp, AX, ADD))
                        ins = ve.tensor_copy(pos[:, k, g * TILES:(g + 1) * TILES], r4[3][:, :])
                        if k == 0:
                            link(ins)
                    ins.then_inc(s["pos_done"], 1)
                    ve.wait_ge(s["pos_done"], g + 1)

            def router():
                ve.wait_ge(s["const_in"], 16 * len(CONSTS))
                ve.tensor_reduce(gsum[:, :], gw[:, :, :].rearrange("p c e -> p e c"), AX, ADD).then_inc(s["gsum_ready"], 1)
                ve.wait_ge(s["gmean_ready"], 1)
                ve.wait_ge(s["gsum_ready"], 1)
                link(ve.tensor_copy(gsum[:, :], bank(S0)[:, 0:E]))
                ve.tensor_tensor(gw[:, :, :], gw[:, :, :], gsum[:, :].rearrange("p (o e) -> p o e", o=1).to_broadcast([P, C, E]), SUB).then_inc(s["gw_ready"], 1)

            def had_low(jj):
                ve.wait_ge(s["had_hi"], jj + 1)
                for a in range(4):
                    ins = ve.scalar_tensor_tensor(w2s[:, 1, 4 * a + jj, :], bank(OUT0 + a), float(H) ** -0.5, w2s[:, 0, 4 * a + jj, :], MUL, SUB)
                ins.then_inc(s["had_lo"], 1)

            def unit_low(u):
                ve.wait_ge(s["unit_hi"], u + 1)
                ve.scalar_tensor_tensor(halves[:, u % 2, 1, :], raw[:, u % 2, :], SW, halves[:, u % 2, 0, :], MUL, SUB).then_inc(s["unit_lo"], 1)

            def chunk(g, j):
                n = J * g + j
                units = slot_units(g, j)
                unit_low(units[0])
                ve.wait_ge(s["sig_done"], n + 1)
                ve.tensor_tensor(sg[:, j % 2, :], bank(ABANK), sg[:, j % 2, :], MUL).then_inc(s["s_done"], 1)
                ve.wait_ge(s["b_done"], n + 1)
                ve.wait_ge(s["s_done"], n + 1)
                ve.scalar_tensor_tensor(sg[:, j % 2, :], sg[:, j % 2, :], SH / (SW * SX) ** 2, bank(BBANK), MUL, MUL).then_inc(s["hid_done"], 1)
                unit_low(units[1])
                ve.wait_ge(s["hh_done"], n + 1)
                ve.tensor_tensor(hs[:, j % 2, 1, :], sg[:, j % 2, :], hs[:, j % 2, 0, :], SUB).then_inc(s["hl_done"], 1)
                for u in units[2:]:
                    unit_low(u)

            def resid(g):
                ve.wait_ge(s["down_done"], J * (g + 1))
                for c in range(C):
                    ins = ve.scalar_tensor_tensor(X[:, g % 3, c, :], bank(OUT0 + c), sc[:, 2:3], X[:, g % 3, c, :], MUL, ADD)
                ins.then_inc(s["resid_done"], 1)
                ve.wait_ge(s["resid_done"], g + 1)

            for item in PROLOGUE:
                if item == "router":
                    router()
                elif isinstance(item, str):
                    run("pre", 0, item)
                elif item[0] == "h":
                    had_low(item[1])
                elif item[0] == "w":
                    ve.wait_ge(s["w_hi"], item[1] + 1)
                    ve.scalar_tensor_tensor(w_dst(item[1], 1), wstage[item[1] % 2], SW, w_dst(item[1], 0), MUL, SUB).then_inc(s["w_lo"], 1)
                else:
                    ve.wait_ge(s["q_hi"], item[1] + 1)
                    ve.scalar_tensor_tensor(q_dst(item[1], 1), qstage[item[1] % 2], SW, q_dst(item[1], 0), MUL, SUB).then_inc(s["q_lo"], 1)
            for g in range(NG):
                if g >= 1:
                    resid(g - 1)
                for j in range(J):
                    chunk(g, j)
                    for step in steps_beside(g, j):
                        run(*step)
            resid(NG - 1)
            for step in EPILOGUE:
                run(*step)

            ve.tensor_copy(a16[:, 0, 0, :], cum[:, :]).then_inc(s["cum_done"], 1)
            ve.wait_ge(s["count_done"], 1)
            link(ve.tensor_copy(cnt[:, 0, :], bank(S1)[:, 0:E]))
            wide16 = cnt[:, 0, :].rearrange("p (e o) -> p e o", o=1).to_broadcast([P, E, 16])
            link(ve.tensor_tensor(cmp16[:, :, :], wide16, blk[:, :].rearrange("p (o j) -> p o j", o=1).to_broadcast([P, E, 16]), ALU.is_gt))
            link(ve.tensor_reduce(cnt[:, 1, :], cmp16[:, :, :], AX, ADD))
            link(ve.memset(cnt[:, 3, :], 1.0))
            link(ve.tensor_tensor_scan(cnt[:, 2, :], cnt[:, 3, :], cnt[:, 1, :], 0.0, MUL, ADD))
            link(ve.tensor_scalar(cnt[:, 4, :], cnt[:, 2, :], 1.0, None, ADD))
            link(ve.tensor_copy(starts[:, :], cnt[:, 4, :]))
            sno3 = sno[:, :].rearrange("p (s o) -> p s o", o=1).to_broadcast([P, SLOTS + 1, E])
            cum3 = cnt[:, 2, :].rearrange("p (o e) -> p o e", o=1).to_broadcast([P, SLOTS + 1, E])
            link(ve.tensor_tensor(sle[:, :, :], sno3, cum3, ALU.is_ge))
            link(ve.tensor_reduce(sl[:, 0, :], sle[:, :, :], AX, ADD))
            link(ve.tensor_tensor(sle[:, :, :], sle[:, :, :], cum3, MUL))
            link(ve.tensor_reduce(sl[:, 1, :], sle[:, :, :], AX, MAXO))
            link(ve.tensor_tensor(sl[:, 2, :], sno[:, :], sl[:, 1, :], SUB))
            link(ve.tensor_scalar(sl[:, 2, :], sl[:, 2, :], float(P), None, MUL))
            link(ve.scalar_tensor_tensor(sl[:, 2, :], sl[:, 0, :], float(TOK), sl[:, 2, :], MUL, ADD))
            link(ve.tensor_copy(table[:, 2, :], sl[:, 2, :]))
            link(ve.tensor_scalar(sl[:, 0, :], sl[:, 0, :], float(E - 1), None, ALU.min))
            link(ve.tensor_copy(table[:, 0, :], sl[:, 0, :]))
            link(ve.tensor_scalar(sl[:, 3, :], sl[:, 0, :], 1.0, 16.0 * (EU // 4), ADD, MUL))
            link(ve.tensor_copy(table[:, 3, :], sl[:, 3, :]))
            link(ve.tensor_scalar(sl[:, 1, :], sl[:, 0, :], 1.0, None, ALU.is_equal))
            for e in range(3, E, 2):
                link(ve.scalar_tensor_tensor(sl[:, 1, :], sl[:, 0, :], float(e), sl[:, 1, :], ALU.is_equal, ADD))
            link(ve.tensor_scalar(sl[:, 1, :], sl[:, 1, :], float(2 * EXPERT), None, MUL))
            ve.tensor_copy(table[:, 1, :], sl[:, 1, :]).then_inc(s["table_done"], 1)

            h1 = PS[:, 0:2, :].rearrange("p b n -> p (b n)")
            h3 = PS[:, 2:4, :].rearrange("p b n -> p (b n)")

            def hidden(i):
                ve.wait_ge(s["sil_done"], i + 1)
                ve.tensor_tensor(sil[0], sil[0], h1, MUL).then_inc(s["g1_done"], 1)
                ve.wait_ge(s["g1_done"], i + 1)
                if not (isinstance(i, int) and i == 0):
                    ve.wait_ge(s["aT_done"], i)
                ve.scalar_tensor_tensor(sil[1], sil[0], SH / (SW * SX) ** 2, h3, MUL, MUL).then_inc(s["act_done"], 1)

            def rows_low(i, par):
                ve.wait_ge(s["xT_used"], i + 1)
                ve.scalar_tensor_tensor(xTt[par][:, 1, :, :], xTp, SX, xTt[par][:, 0, :, :], MUL, SUB).then_inc(s["xTl_done"], 1)

            def hidden_low(i, par):
                ve.wait_ge(s["aT_used"], i + 1)
                ve.tensor_tensor(aTt[par][:, 1, :, :], aTp, aTt[par][:, 0, :, :], SUB).then_inc(s["aTl_done"], 1)

            def evac_y(i, n, par):
                ve.wait_ge(s["slot_down"], i + 2)
                ve.wait_ge(out_s[par], 16 * n)
                ve.tensor_scalar(yt[par], bank(7), outl_w[:, par, 1:2], None, MUL).then_inc(s["y_ready"], 1)

            ve.memset(cnt[:, 5, 0:1], 0.0).then_inc(s["act_done"], 1)
            ve.memset(cnt[:, 5, 1:2], 0.0).then_inc(s["y_ready"], 1)
            rows_low(0, 0)
            hidden(0)
            rows_low(1, 1)
            hidden_low(0, 0)
            for i in (1, 2):
                hidden(i)
                rows_low(i + 1, 1 - i % 2)
                evac_y(i - 1, 1, 1 - i % 2)
                hidden_low(i, i % 2)
            with ve.Fori(1, (SLOTS - 1) // 2, 1) as m:
                for par in (1, 0):
                    i = 2 * m + 2 - par
                    hidden(i)
                    rows_low(i + 1, 1 - par)
                    ve.wait_ge(ysto[1 - par], 16 * m)
                    evac_y(i - 1, m + 1, 1 - par)
                    hidden_low(i, par)
            ve.wait_ge(ysto[0], 16 * ((SLOTS - 1) // 2))
            evac_y(SLOTS - 1, (SLOTS + 1) // 2, 0)
        @blockv.tensor
        def _(te):
            PAIRS = ((0, 0), (0, 1), (1, 0))

            def run(kind, g, step):
                b = branch_index(kind, g)
                second = step.endswith("2")
                if step in ("sums", "sums2"):
                    n = norm_index(kind, g, int(second))
                    te.wait_ge(s["sums_done"], n + 1)
                    te.wait_ge(s["xsum_done"], n + 1)
                    if n >= 1:
                        te.wait_ge(s["var_done"], n)
                    norms_taken[0] = n + 1
                    te.matmul(bank(S0), onesm[:, :], E2[:, 2 * NT:3 * NT], start=True, stop=True)
                    te.matmul(bank(S1), onesm[:, :], E2[:, 3 * NT:4 * NT], start=True, stop=True).then_inc(s["stat_done"], 1)
                elif step == "rows":
                    te.wait_ge(s["wkv_done"], b + 1)
                    te.wait_ge(s["gw_ready"], 1)
                    xv = X[:, g % 3, :, :]
                    for i in range(TILES):
                        for c in range(C):
                            ins = te.matmul(bank(S1)[:, i * E:(i + 1) * E], xv[:, c, i * P:(i + 1) * P], gw[:, c, :], start=(c == 0), stop=(c == C - 1))
                    ins.then_inc(s["lg_done"], 1)
                    for i in range(TILES):
                        if i == 1:
                            te.wait_ge(s["raw_done"], g + 1)
                        if i >= 2:
                            te.wait_ge(s["xt_done"], TILES * g + i - 1)
                        for c in range(C):
                            ins = te.transpose(bank(S0 + i % 2)[:, c * P:(c + 1) * P], xv[:, c, i * P:(i + 1) * P], idn[:, :])
                        ins.then_inc(s["tr_done"], 1)
                elif step == "rank":
                    te.wait_ge(s["asg_done"], g + 1)
                    te.wait_ge(s["var_done"], norms_taken[0])
                    te.wait_ge(s["xt_done"], TILES * (g + 1))
                    for i in range(TILES):
                        o = bank(S0)[:, i * E:(i + 1) * E]
                        te.matmul(o, tris[:, :], a16[:, 0, i, :], start=True, stop=False)
                        ins = te.matmul(o, ones1[:, :], a16[:, 1, i, :], start=False, stop=True)
                    ins.then_inc(s["rank_done"], 1)

            norms_taken = [0]

            def up(g, j):
                for bk, w, sem_, free in ((ABANK, w1s, "a_done", "s_done"), (BBANK, w3s, "b_done", "hid_done")):
                    if not (isinstance(j, int) and J * g + j == 0):
                        te.wait_ge(s[free], J * g + j)
                    for n, (a, b) in enumerate(PAIRS):
                        for c in range(C):
                            ins = te.matmul(bank(bk), w[:, a, c, bass.ds(j * P, P)], xs[:, g % 2, b, c, :],
                                            start=(n == 0 and c == 0), stop=(n == 2 and c == C - 1))
                    ins.then_inc(s[sem_], 1)

            def down(g, j, par):
                te.wait_ge(s["hl_done"], J * g + j + 1)
                first, last = isinstance(j, int) and j == 0, isinstance(j, int) and j == J - 1
                if first and g >= 1:
                    te.wait_ge(s["resid_done"], g)
                for c in range(C):
                    for n, (a, b) in enumerate(PAIRS):
                        ins = te.matmul(bank(OUT0 + c), w2s[:, a, j, c * P:(c + 1) * P], hs[:, par, b, :],
                                        start=first and n == 0, stop=last and n == 2)
                ins.then_inc(s["down_done"], 1)
                return ins

            te.wait_ge(s["hot_in"], 48)
            for item in PROLOGUE:
                if item == "router":
                    te.wait_ge(s["gsum_ready"], 1)
                    te.wait_ge(s["var_done"], 1)
                    te.matmul(bank(S0)[:, 0:E], onesm[:, :], gsum[:, :], start=True, stop=True).then_inc(s["gmean_ready"], 1)
                elif isinstance(item, str):
                    if item == "sums2":
                        te.wait_ge(s["gw_ready"], 1)
                    run("pre", 0, item)
                elif item[0] == "h":
                    jj = item[1]
                    if jj == 0:
                        te.wait_ge(s["const_in"], 16 * len(CONSTS))
                        te.wait_ge(s["q_lo"], NQ)
                    else:
                        te.wait_ge(s["had_lo"], jj)
                    for a in range(4):
                        for n, (k, half) in enumerate((k, half) for k in range(4) for half in range(2)):
                            sign = bin(a & k).count("1") % 2
                            ins = te.matmul(bank(OUT0 + a), hads[:, sign, :], w2s[:, half, 4 * k + jj, :], start=(n == 0), stop=(n == 7))
                    ins.then_inc(s["had_out"], 1)
            te.wait_ge(s["had_lo"], 4)
            te.wait_ge(s["w_lo"], NW)
            te.wait_ge(s["gw_ready"], 1)
            for g in range(NG):
                te.wait_ge(s["xs_ready"], g + 1)
                up(g, 0)
                for j in range(1, J):
                    up(g, j)
                    down(g, j - 1, (j - 1) % 2)
                    for step in steps_beside(g, j - 1):
                        run(*step)
                down(g, J - 1, (J - 1) % 2)
                for step in steps_beside(g, J - 1):
                    run(*step)
            for step in EPILOGUE:
                run(*step)
            te.wait_ge(s["cum_done"], 1)
            te.matmul(bank(S1)[:, 0:E], ones1[:, :], a16[:, 0, 0, :], start=True, stop=True).then_inc(s["count_done"], 1)

            te.wait_ge(s["table_done"], 1)
            load = lambda row, i, top: te.value_load(table[0:1, row, bass.ds(i, 1)], min_val=0, max_val=top)

            def rows_t(i, n, par):
                te.wait_ge(row_s[par], 16 * n)
                if not (isinstance(i, int) and i == 0):
                    te.wait_ge(s["xTl_done"], i)
                for c in range(C):
                    ins = te.transpose(bank(4)[:, c * P:(c + 1) * P], grow[par][:, c * P:(c + 1) * P], idn[:, :])
                    if isinstance(i, int) and i == 0 and c == 0:
                        ins.then_inc(s["slot_down"], 1)
                ins.then_inc(s["xT_done"], 1)

            ROWS_FIRST = ((0, 0), (0, 1), (1, 0))

            def weights_of(off, unit, half):
                return w16[:, bass.ds(off + (2 * unit + half) * U, U)]

            def experts_up(i, par):
                loads, off = load(3, i, 16 * (EU // 4) * E), load(1, i, 2 * EXPERT)
                te.wait_ge(wl[0], loads)
                te.wait_ge(wl[1], loads)
                te.wait_ge(s["xTl_done"], i + 1)
                te.wait_ge(s["act_done"], i + 1)
                for c in range(C):
                    for k, (b, a) in enumerate(ROWS_FIRST):
                        for n in range(2 * I // NT):
                            ins = te.matmul(bank(n), xTt[par][:, b, c, :], weights_of(off, 2 * I // NT * c + n, a),
                                            start=(c == 0 and k == 0), stop=(c == C - 1 and k == 2))
                ins.then_inc(s["up_done"], 1)

            def experts_down(i, par):
                off = load(1, i, 2 * EXPERT)
                te.wait_ge(s["aTl_done"], i + 1)
                te.wait_ge(s["y_ready"], i + 1)
                for c in range(IC):
                    for k, (b, a) in enumerate(ROWS_FIRST):
                        ins = te.matmul(bank(7), aTt[par][:, b, c, :], weights_of(off, 2 * C * I // U + c, a),
                                        start=(c == 0 and k == 0), stop=(c == IC - 1 and k == 2))
                ins.then_inc(s["slot_down"], 1)

            def hidden_t(i):
                te.wait_ge(s["act_done"], i + 2)
                if not (isinstance(i, int) and i == 0):
                    te.wait_ge(s["aTl_done"], i)
                for c in range(IC):
                    ins = te.transpose(bank(5 + c // C)[:, c % C * P:(c % C + 1) * P], sil[1][:, c * P:(c + 1) * P], idn[:, :])
                ins.then_inc(s["aT_done"], 1)

            def block(i, n, par):
                experts_up(i, par)
                rows_t(i + 1, n, 1 - par)
                if not (isinstance(i, int) and i == 0):
                    experts_down(i - 1, 1 - par)
                hidden_t(i)

            rows_t(0, 1, 0)
            block(0, 1, 0)
            with te.Fori(0, (SLOTS - 1) // 2, 1) as m:
                block(2 * m + 1, m + 2, 1)
                block(2 * m + 2, m + 2, 0)
            experts_down(SLOTS - 1, 0)


def kernel(**inputs):
    import numpy as np
    import concourse.bacc as bacc
    from concourse.bass_utils import run_bass_kernel_spmd as launch

    a = {k: np.asarray(v) for k, v in inputs.items()}

    def channel_major(v):
        return v.reshape(NG, NB, T, C, P).transpose(0, 4, 3, 1, 2).reshape(NG, P, W)

    def cols(v):
        return v.reshape(C, P).T

    def rows_first(w, chunks):
        return w.T.reshape(chunks, P, w.shape[0]).transpose(1, 0, 2)

    h = np.array([[1.0]], np.float32)
    while h.shape[0] < P:
        h = np.block([[h, h], [h, -h]])
    lower = np.arange(P)
    wide = lambda v, dt: np.broadcast_to(np.asarray(v, dt), (P, len(v)))
    w1 = a["L1_ffn_w1"].transpose(0, 2, 1).reshape(E, C, P, I)
    w3 = a["L1_ffn_w3"].transpose(0, 2, 1).reshape(E, C, P, I)
    arrays = {
        "x_cm": channel_major(a["x"]),
        "ctx_cm": channel_major(a["ctx_2048"]),
        "vecs": np.stack([cols(a[n]) for n in ("L0_xattn_w", "L0_xattn_u", "L1_xattn_time_decay", "L1_xattn_time_first")], 1),
        "gains": np.broadcast_to(np.concatenate([a["g_xattn"], a["g_ffn"]]), (P, 4)),
        "w1t": rows_first(a["L0_ffn_W1"], C),
        "w3t": rows_first(a["L0_ffn_W3"], C),
        "w2t": rows_first(a["L0_ffn_W2"], J),
        "gate_t": rows_first(a["L1_ffn_gate_w"], C),
        "ew": np.concatenate([
            np.concatenate([w1, w3], 3).reshape(E, C, P, 2 * I // U, U).transpose(0, 1, 3, 2, 4).reshape(E, -1, P, U),
            a["L1_ffn_w2"].transpose(0, 2, 1).reshape(E, IC, P, D)], 1).reshape(NU * P, U),
        "had": np.stack([h, -h], 1).astype(np.float16),
        "ones_mean": np.full((P, P), 1.0 / D, np.float32),
        "ident": np.eye(P, dtype=np.float32),
        "tri": (lower[:, None] < lower[None, :]).astype(np.float16),
        "ones16": np.ones((P, P), np.float16),
        "tok_id": np.stack([np.broadcast_to(lower[:, None] + P * np.arange(TOK // P), (2, P, TOK // P)).transpose(1, 0, 2),
                            np.zeros((P, 2, TOK // P), np.int64)], 3).astype(np.int32),
        "ebase": wide(TOK * np.arange(E), np.float32),
        "desc": wide(E - np.arange(E), np.float32),
        "blocks": wide(P * np.arange(16), np.float32),
        "slot_no": wide(np.arange(SLOTS + 1), np.float32),
        "spare_rows": np.stack([TOK + np.arange(LIST) % P, np.zeros(LIST, np.int64)], 1).astype(np.int32).reshape(P, 2 * LIST // P),
        "zero_rows": np.zeros((P, D), np.float32),
    }
    arrays = {k: np.ascontiguousarray(v) for k, v in arrays.items()}
    nc = bacc.Bacc("TRN2", target_bir_lowering=False, num_devices=1)
    args = [nc.dram_tensor(n, v.shape, mybir.dt.from_np(v.dtype), kind="ExternalInput").ap() for n, v in arrays.items()]
    out = nc.dram_tensor("out", (TOK + P, D), F32, kind="ExternalOutput").ap()
    build(nc, *args, out)
    r = launch(nc, [arrays], core_ids=[0])
    return r.results[0]["out"][:TOK].reshape(BATCH, T, D)
```
